# Optimizing a Trainium2 kernel written in Bass

```python
import numpy as np
import jax
import jax.numpy as jnp

def _softmax(x, axis=-1):
    return jax.nn.softmax(x, axis=axis)

def _gelu(x):
    return jax.nn.gelu(x, approximate=True)

def _silu(x):
    return jax.nn.silu(x)

def _sigmoid(x):
    return jax.nn.sigmoid(x)

def _layernorm(x, axis=-1, eps=1e-05):
    m = jnp.mean(x, axis=axis, keepdims=True)
    v = jnp.var(x, axis=axis, keepdims=True)
    return (x - m) / jnp.sqrt(v + eps)

def _scatter_add(tgt, idx, src, axis=0):
    return tgt.at[idx].add(src)

def _segment_sum(src, seg, n):
    return jax.ops.segment_sum(src, seg, n)
kernel_name = 'mk_decoder_postln_d1_seqx_r8_b9194e'

def setup_inputs(seed: int=0):
    np.random.seed(seed)
    _w = jnp.asarray

    def _rec_inputs():
        import jax
        import jax.numpy as jnp
        _rk = jax.random.key(seed)
        x = 7.22e-05 + 1 * jax.random.normal(jax.random.fold_in(_rk, 1), (1, 1024, 128), jnp.float32)
        _lenS = 1024 - jax.random.randint(jax.random.fold_in(_rk, 7), (1,), 0, max(1, 1024 // 4) + 1, jnp.int32)
        _lenS2 = 6404 - jax.random.randint(jax.random.fold_in(_rk, 8), (1,), 0, max(1, 6404 // 4) + 1, jnp.int32)
        _ctx_768P = jax.random.normal(jax.random.fold_in(_rk, 11), (1, 16, 96), jnp.float32)
        _ctx_768c = jax.random.dirichlet(jax.random.fold_in(_rk, 511), 0.3 * jnp.ones((16,), jnp.float32), (1, 6404))
        _ctx_768t = jnp.einsum('bsk,bkd->bsd', _ctx_768c, _ctx_768P)
        _ctx_768t = _ctx_768t * jax.lax.rsqrt(jnp.mean(jnp.square(_ctx_768t)) + 1e-12) * 0.953939
        ctx_768 = 2.09791e-05 + 1.00001 * (_ctx_768t + 0.3 * jax.random.normal(jax.random.fold_in(_rk, 611), (1, 6404, 96), jnp.float32))
        return (x, ctx_768)
    x, ctx_768 = _rec_inputs()

    def _L0_attn_setup():
        import jax, jax.numpy as jnp
        import numpy as np
        from jax import lax
        B, S, D = (4, 256, 128)
        L, H, K = (4, 4, 4)
        DH = D // H
        UP = 168
        EPS = 1e-05

        def _ln(x, w):
            mu = x.mean(-1, keepdims=True)
            var = x.var(-1, keepdims=True)
            return (x - mu) * lax.rsqrt(var + EPS) * w

        def _slstm_layer(xn, cw, cb, wi, wf, wz, wo, rk, b, gnw):
            Bc, Sc, Dc = xn.shape
            xc = lax.conv_general_dilated(xn.transpose(0, 2, 1), cw[:, None, :], (1,), [(K - 1, 0)], dimension_numbers=('NCH', 'OIH', 'NCH'), feature_group_count=Dc)
            xc = jax.nn.silu(xc + cb[None, :, None]).transpose(0, 2, 1)
            hx = xc.reshape(Bc, Sc, H, DH)
            hz = xn.reshape(Bc, Sc, H, DH)
            gi = jnp.einsum('bshd,hod->bsho', hx, wi)
            gf = jnp.einsum('bshd,hod->bsho', hx, wf)
            gz = jnp.einsum('bshd,hod->bsho', hz, wz)
            go = jnp.einsum('bshd,hod->bsho', hz, wo)
            wx = jnp.stack([gi, gf, gz, go], axis=3)

            def step(carry, wx_t):
                h, c, n, m = carry
                raw = wx_t + jnp.einsum('bhd,hdgo->bhgo', h, rk) + b
                ir, fr, zr, og = (raw[:, :, 0], raw[:, :, 1], raw[:, :, 2], raw[:, :, 3])
                lfm = m + jax.nn.log_sigmoid(fr)
                mn = jnp.maximum(ir, lfm)
                ig = jnp.exp(ir - mn)
                fg = jnp.exp(lfm - mn)
                cn = fg * c + ig * jnp.tanh(zr)
                nn = fg * n + ig
                hn = jax.nn.sigmoid(og) * cn / nn
                return ((hn, cn, nn, mn), hn)
            z0 = jnp.zeros((Bc, H, DH), xn.dtype)
            _, ys = lax.scan(step, (z0, z0, z0, z0), jnp.moveaxis(wx, 1, 0))
            y = jnp.moveaxis(ys, 0, 1)
            mu = y.mean(-1, keepdims=True)
            var = y.var(-1, keepdims=True)
            y = (y - mu) * lax.rsqrt(var + EPS) * gnw.reshape(H, DH)
            return y.reshape(Bc, Sc, Dc)

        def _ffn(xn, wu, wd):
            u = xn @ wu
            g, v = (u[..., :UP], u[..., UP:])
            return jax.nn.gelu(g, approximate=False) * v @ wd
        key = jax.random.key(seed)
        ks = jax.random.split(key, 9)
        sg = DH ** (-0.5)
        return {'x': jax.random.normal(ks[0], (B, S, D), jnp.float32), 'ln1_w': jnp.ones((L, D), jnp.float32), 'conv_w': jax.random.normal(ks[1], (L, D, K), jnp.float32) * 0.1, 'conv_b': jnp.zeros((L, D), jnp.float32), 'wi': jax.random.normal(ks[2], (L, H, DH, DH), jnp.float32) * sg, 'wf': jax.random.normal(ks[3], (L, H, DH, DH), jnp.float32) * sg, 'wz': jax.random.normal(ks[4], (L, H, DH, DH), jnp.float32) * sg, 'wo': jax.random.normal(ks[5], (L, H, DH, DH), jnp.float32) * sg, 'rker': jax.random.normal(ks[6], (L, H, DH, 4, DH), jnp.float32) * sg, 'cell_b': jax.random.normal(ks[7], (L, H, 4, DH), jnp.float32) * 0.1, 'gn_w': jnp.ones((L, D), jnp.float32), 'ln2_w': jnp.ones((L, D), jnp.float32), 'ff_up': jax.random.normal(ks[8], (L, D, 2 * UP), jnp.float32) * D ** (-0.5), 'ff_down': jax.random.normal(jax.random.fold_in(key, 99), (L, UP, D), jnp.float32) * UP ** (-0.5), 'post_w': jnp.ones((D,), jnp.float32)}
    _L0_attn_all = _L0_attn_setup()
    _L0_attn_in = {k: v for k, v in _L0_attn_all.items() if k in ('ln1_w', 'conv_w', 'conv_b', 'wi', 'wf', 'wz', 'wo', 'rker', 'cell_b', 'gn_w', 'ln2_w', 'ff_up', 'ff_down', 'post_w')}
    del _L0_attn_all

    def _L0_xattn_setup():
        import jax, jax.numpy as jnp
        import numpy as np
        HEADS = 16
        DIM_HEAD = 64
        key = jax.random.key(seed)
        ks = jax.random.split(key, 7)
        B, Nq, Dq = (4, 256, 128)
        Nk, Dc = (128, 96)
        inner = HEADS * DIM_HEAD
        sq = 1.0 / np.sqrt(Dq)
        sc = 1.0 / np.sqrt(Dc)
        si = 1.0 / np.sqrt(inner)
        return {'x': jax.random.normal(ks[0], (B, Nq, Dq), dtype=jnp.float32), 'context': jax.random.normal(ks[1], (B, Nk, Dc), dtype=jnp.float32), 'Wq': jax.random.normal(ks[2], (Dq, inner), dtype=jnp.float32) * sq, 'Wk': jax.random.normal(ks[3], (Dc, inner), dtype=jnp.float32) * sc, 'Wv': jax.random.normal(ks[4], (Dc, inner), dtype=jnp.float32) * sc, 'Wo': jax.random.normal(ks[5], (inner, Dq), dtype=jnp.float32) * si, 'bo': jax.random.normal(ks[6], (Dq,), dtype=jnp.float32) * 0.01}
    _L0_xattn_all = _L0_xattn_setup()
    _L0_xattn_in = {k: v for k, v in _L0_xattn_all.items() if k in ('Wq', 'Wk', 'Wv', 'Wo', 'bo')}
    del _L0_xattn_all

    def _L0_ffn_setup():
        import math
        import jax, jax.numpy as jnp
        import numpy as np
        D_MODEL = 128
        D_FF = 512
        N_EXPERTS = 8
        CAPACITY_FACTOR = 1.25
        L, B = (64, 8)

        def _route(tokens, router_w):
            T = tokens.shape[0]
            E = router_w.shape[0]
            capacity = int(math.ceil(T / E * CAPACITY_FACTOR))
            logits = tokens @ router_w.T
            probs = jax.nn.softmax(logits, axis=-1)
            top1_idx = jnp.argmax(probs, axis=-1)
            top1_prob = jnp.max(probs, axis=-1)
            order = jnp.lexsort((-top1_prob, top1_idx))
            sorted_e = top1_idx[order]
            counts = jnp.bincount(top1_idx, length=E)
            start = jnp.cumsum(counts) - counts
            pos_in_group = jnp.arange(T) - start[sorted_e]
            keep_sorted = pos_in_group < capacity
            keep = jnp.zeros((T,), bool).at[order].set(keep_sorted)
            return jnp.where(keep, top1_idx, 0).astype(jnp.int32)
        key = jax.random.key(seed)
        ks = jax.random.split(key, 6)
        s_in = 1.0 / math.sqrt(D_MODEL)
        s_ff = 1.0 / math.sqrt(D_FF)
        return {'x': jax.random.normal(ks[0], (L, B, D_MODEL), dtype=jnp.float32), 'router_w': jax.random.uniform(ks[1], (N_EXPERTS, D_MODEL), minval=-s_in, maxval=s_in), 'W1': jax.random.uniform(ks[2], (N_EXPERTS, D_MODEL, D_FF), minval=-s_in, maxval=s_in), 'b1': jax.random.uniform(ks[3], (N_EXPERTS, D_FF), minval=-s_in, maxval=s_in), 'W2': jax.random.uniform(ks[4], (N_EXPERTS, D_FF, D_MODEL), minval=-s_ff, maxval=s_ff), 'b2': jax.random.uniform(ks[5], (N_EXPERTS, D_MODEL), minval=-s_ff, maxval=s_ff)}
    _L0_ffn_all = _L0_ffn_setup()
    _L0_ffn_in = {k: v for k, v in _L0_ffn_all.items() if k in ('router_w', 'W1', 'b1', 'W2', 'b2')}
    del _L0_ffn_all
    return {'x': x, 'ctx_768': ctx_768, 'L0_attn_ln1_w': _L0_attn_in['ln1_w'], 'L0_attn_conv_w': _L0_attn_in['conv_w'], 'L0_attn_conv_b': _L0_attn_in['conv_b'], 'L0_attn_wi': _L0_attn_in['wi'], 'L0_attn_wf': _L0_attn_in['wf'], 'L0_attn_wz': _L0_attn_in['wz'], 'L0_attn_wo': _L0_attn_in['wo'], 'L0_attn_rker': _L0_attn_in['rker'], 'L0_attn_cell_b': _L0_attn_in['cell_b'], 'L0_attn_gn_w': _L0_attn_in['gn_w'], 'L0_attn_ln2_w': _L0_attn_in['ln2_w'], 'L0_attn_ff_up': _L0_attn_in['ff_up'], 'L0_attn_ff_down': _L0_attn_in['ff_down'], 'L0_attn_post_w': _L0_attn_in['post_w'], 'L0_xattn_Wq': _L0_xattn_in['Wq'], 'L0_xattn_Wk': _L0_xattn_in['Wk'], 'L0_xattn_Wv': _L0_xattn_in['Wv'], 'L0_xattn_Wo': _L0_xattn_in['Wo'], 'L0_xattn_bo': _L0_xattn_in['bo'], 'L0_ffn_router_w': _L0_ffn_in['router_w'], 'L0_ffn_W1': _L0_ffn_in['W1'], 'L0_ffn_b1': _L0_ffn_in['b1'], 'L0_ffn_W2': _L0_ffn_in['W2'], 'L0_ffn_b2': _L0_ffn_in['b2']}

def reference(x, ctx_768, L0_attn_ln1_w, L0_attn_conv_w, L0_attn_conv_b, L0_attn_wi, L0_attn_wf, L0_attn_wz, L0_attn_wo, L0_attn_rker, L0_attn_cell_b, L0_attn_gn_w, L0_attn_ln2_w, L0_attn_ff_up, L0_attn_ff_down, L0_attn_post_w, L0_xattn_Wq, L0_xattn_Wk, L0_xattn_Wv, L0_xattn_Wo, L0_xattn_bo, L0_ffn_router_w, L0_ffn_W1, L0_ffn_b1, L0_ffn_W2, L0_ffn_b2):
    import jax
    import jax.numpy as jnp

    def _L0_attn_ref(x, ln1_w, conv_w, conv_b, wi, wf, wz, wo, rker, cell_b, gn_w, ln2_w, ff_up, ff_down, post_w):
        import jax, jax.numpy as jnp
        import numpy as np
        from jax import lax
        B, S, D = (4, 256, 128)
        L, H, K = (4, 4, 4)
        DH = D // H
        UP = 168
        EPS = 1e-05

        def _ln(x, w):
            mu = x.mean(-1, keepdims=True)
            var = x.var(-1, keepdims=True)
            return (x - mu) * lax.rsqrt(var + EPS) * w

        def _slstm_layer(xn, cw, cb, wi, wf, wz, wo, rk, b, gnw):
            Bc, Sc, Dc = xn.shape
            xc = lax.conv_general_dilated(xn.transpose(0, 2, 1), cw[:, None, :], (1,), [(K - 1, 0)], dimension_numbers=('NCH', 'OIH', 'NCH'), feature_group_count=Dc)
            xc = jax.nn.silu(xc + cb[None, :, None]).transpose(0, 2, 1)
            hx = xc.reshape(Bc, Sc, H, DH)
            hz = xn.reshape(Bc, Sc, H, DH)
            gi = jnp.einsum('bshd,hod->bsho', hx, wi)
            gf = jnp.einsum('bshd,hod->bsho', hx, wf)
            gz = jnp.einsum('bshd,hod->bsho', hz, wz)
            go = jnp.einsum('bshd,hod->bsho', hz, wo)
            wx = jnp.stack([gi, gf, gz, go], axis=3)

            def step(carry, wx_t):
                h, c, n, m = carry
                raw = wx_t + jnp.einsum('bhd,hdgo->bhgo', h, rk) + b
                ir, fr, zr, og = (raw[:, :, 0], raw[:, :, 1], raw[:, :, 2], raw[:, :, 3])
                lfm = m + jax.nn.log_sigmoid(fr)
                mn = jnp.maximum(ir, lfm)
                ig = jnp.exp(ir - mn)
                fg = jnp.exp(lfm - mn)
                cn = fg * c + ig * jnp.tanh(zr)
                nn = fg * n + ig
                hn = jax.nn.sigmoid(og) * cn / nn
                return ((hn, cn, nn, mn), hn)
            z0 = jnp.zeros((Bc, H, DH), xn.dtype)
            _, ys = lax.scan(step, (z0, z0, z0, z0), jnp.moveaxis(wx, 1, 0))
            y = jnp.moveaxis(ys, 0, 1)
            mu = y.mean(-1, keepdims=True)
            var = y.var(-1, keepdims=True)
            y = (y - mu) * lax.rsqrt(var + EPS) * gnw.reshape(H, DH)
            return y.reshape(Bc, Sc, Dc)

        def _ffn(xn, wu, wd):
            u = xn @ wu
            g, v = (u[..., :UP], u[..., UP:])
            return jax.nn.gelu(g, approximate=False) * v @ wd
        for l in range(L):
            x = x + _slstm_layer(_ln(x, ln1_w[l]), conv_w[l], conv_b[l], wi[l], wf[l], wz[l], wo[l], rker[l], cell_b[l], gn_w[l])
            x = x + _ffn(_ln(x, ln2_w[l]), ff_up[l], ff_down[l])
        return _ln(x, post_w)

    def _L0_xattn_ref(x, context, Wq, Wk, Wv, Wo, bo):
        import jax, jax.numpy as jnp
        import numpy as np
        HEADS = 16
        DIM_HEAD = 64
        B, Nq, _ = x.shape
        Nk = context.shape[1]
        h, dh = (HEADS, DIM_HEAD)
        q = (x @ Wq).reshape(B, Nq, h, dh)
        k = (context @ Wk).reshape(B, Nk, h, dh)
        v = (context @ Wv).reshape(B, Nk, h, dh)
        scale = 1.0 / jnp.sqrt(jnp.asarray(dh, dtype=x.dtype))
        scores = jnp.einsum('bqhd,bkhd->bhqk', q, k) * scale
        attn = jax.nn.softmax(scores, axis=-1)
        out = jnp.einsum('bhqk,bkhd->bqhd', attn, v).reshape(B, Nq, h * dh)
        return out @ Wo + bo

    def _L0_ffn_ref(x, router_w, W1, b1, W2, b2):
        import math
        import jax, jax.numpy as jnp
        import numpy as np
        D_MODEL = 128
        D_FF = 512
        N_EXPERTS = 8
        CAPACITY_FACTOR = 1.25
        L, B = (64, 8)

        def _route(tokens, router_w):
            T = tokens.shape[0]
            E = router_w.shape[0]
            capacity = int(math.ceil(T / E * CAPACITY_FACTOR))
            logits = tokens @ router_w.T
            probs = jax.nn.softmax(logits, axis=-1)
            top1_idx = jnp.argmax(probs, axis=-1)
            top1_prob = jnp.max(probs, axis=-1)
            order = jnp.lexsort((-top1_prob, top1_idx))
            sorted_e = top1_idx[order]
            counts = jnp.bincount(top1_idx, length=E)
            start = jnp.cumsum(counts) - counts
            pos_in_group = jnp.arange(T) - start[sorted_e]
            keep_sorted = pos_in_group < capacity
            keep = jnp.zeros((T,), bool).at[order].set(keep_sorted)
            return jnp.where(keep, top1_idx, 0).astype(jnp.int32)
        Lx, Bx, D = x.shape
        T = Lx * Bx
        E = router_w.shape[0]
        tokens = x.reshape(T, D)
        final_e = _route(tokens, router_w)
        out = jnp.zeros_like(tokens)
        for e in range(E):
            h = jax.nn.relu(tokens @ W1[e] + b1[e])
            y = h @ W2[e] + b2[e]
            out = out + jnp.where((final_e == e)[:, None], y, 0.0)
        return out.reshape(Lx, Bx, D)
    x = _layernorm(x + _L0_attn_ref(x, L0_attn_ln1_w, L0_attn_conv_w, L0_attn_conv_b, L0_attn_wi, L0_attn_wf, L0_attn_wz, L0_attn_wo, L0_attn_rker, L0_attn_cell_b, L0_attn_gn_w, L0_attn_ln2_w, L0_attn_ff_up, L0_attn_ff_down, L0_attn_post_w), axis=-1)
    x = _layernorm(x + _L0_xattn_ref(x, ctx_768, L0_xattn_Wq, L0_xattn_Wk, L0_xattn_Wv, L0_xattn_Wo, L0_xattn_bo), axis=-1)
    x = _layernorm(x + _L0_ffn_ref(x, L0_ffn_router_w, L0_ffn_W1, L0_ffn_b1, L0_ffn_W2, L0_ffn_b2), axis=-1)
    return x

_drawn_inputs = setup_inputs


def setup_inputs(seed=0):
    import zlib

    import numpy as np

    out = dict(_drawn_inputs(seed))
    spreads = {'L0_attn_ln1_w': (1.0, 0.2),
     'L0_attn_conv_b': (0.0, 0.1),
     'L0_attn_gn_w': (1.0, 0.2),
     'L0_attn_ln2_w': (1.0, 0.2),
     'L0_attn_post_w': (1.0, 0.2)}
    factors = {'L0_ffn_b1': 2.808}
    for name, (base, spread) in spreads.items():
        noise = np.random.default_rng([zlib.crc32(name.encode()), seed]).standard_normal(out[name].shape)
        drawn = base * np.exp(spread * noise) if base else spread * noise
        out[name] = jnp.asarray(drawn.astype(out[name].dtype))
    for name, factor in factors.items():
        out[name] = (out[name] * factor).astype(out[name].dtype)
    return out
```

```python
from contextlib import ExitStack

import numpy as np
import concourse.bass as bass
from concourse import mybir

ALU = mybir.AluOpType
ACT = mybir.ActivationFunctionType
AX_X = mybir.AxisListType.X
F32 = mybir.dt.float32
F16 = mybir.dt.float16
BF16 = mybir.dt.bfloat16

P = 128
Q = 32
EPS = 1e-5
H_SCALE = 2.0 ** 12
R_SCALE = 2.0 ** 8
G_SCALE = H_SCALE * R_SCALE
M_SCALE = 2.0 ** 6
M_START = -32.0
LN_LOW = 2.0 ** -63
E_TOP = 2.0 ** 40


def slstm_stage(nc, x, w, scratch_in, scratch_out, dims):
    S, D, L, H, K, UP = dims
    DH = D // H
    CH = P // L
    C = L * H
    LAG = 2
    NCH = S // CH
    ITERS = NCH + LAG * (L - 1)
    assert ITERS % 2 == 0
    assert DH == Q and CH == Q and D == P and CH * C == 512

    with ExitStack() as ctx:
        def sb(name, shape, dt=F32):
            return ctx.enter_context(nc.sbuf_tensor(name, shape, dt))

        def ps(name, shape, dt=F32):
            return ctx.enter_context(nc.psum_tensor(name, shape, dt))

        sems = []

        def sem(name):
            s = ctx.enter_context(nc.semaphore(name))
            sems.append(s)
            return s

        ident = sb("ident", [P, P])
        gate_w = sb("gate_w", [P, L, H, 4, Q])
        gate_b = sb("gate_b", [P, 4, Q])
        pick = sb("pick", [P, CH, C])
        rec_w = sb("rec_w", [P, C, P], F16)
        m_eye = sb("m_eye", [P, P], F16)
        up_w = sb("up_w", [P, L, 2 * UP])
        dn_w0 = sb("dn_w0", [P, L, D])
        dn_w1 = sb("dn_w1", [UP - P, L, D])
        conv_w = sb("conv_w", [P, L, K])
        conv_b = sb("conv_b", [P, L])
        ln1_w = sb("ln1_w", [P, L])
        ln2_w = sb("ln2_w", [P, L])
        gn_w = sb("gn_w", [P, D])
        eps_ln = sb("eps_ln", [P, 1])
        eps_gn = sb("eps_gn", [P, 1])
        keep = sb("keep", [P, ITERS + 1, C])
        xin = [sb(f"xin{i}", [P, D]) for i in range(2)]
        x1 = sb("x1", [P, D])
        x2 = sb("x2", [P, D])
        stats = sb("stats", [P, 6])
        mv = sb("mv", [P, 2])
        lnv = sb("lnv", [P, H])
        rstd = sb("rstd", [P, H])
        normed = sb("normed", [P, D])
        xn = sb("xn", [P, L, K - 1 + CH])
        taps = sb("taps", [P, K, L, CH])
        cv = sb("cv", [P, L, CH])
        cv2 = sb("cv2", [P, L, CH])
        sg = sb("sg", [P, L, CH])
        sg1 = sb("sg1", [P, L, CH])
        sr = sb("sr", [P, L, CH])
        xc = sb("xc", [P, L, CH])
        yt = sb("yt", [P, H, Q])
        yc = sb("yc", [P, H, Q])
        ysq = sb("ysq", [P, H, Q])
        ysum = sb("ysum", [P, H])
        yvar = sb("yvar", [P, H])
        yg = sb("yg", [P, D])
        n2t = sb("n2t", [P, L, CH])
        gl = sb("gl", [P, UP])
        act = sb("act", [P, UP])
        at0 = sb("at0", [P, P])
        at1 = sb("at1", [UP - P, P])
        eb = sb("eb", [Q, C])
        ex = sb("ex", [Q, 3 * C])
        ad = sb("ad", [Q, 3 * C])
        tt = sb("tt", [Q, 3 * C])
        p1 = sb("p1", [Q, C])
        p2 = sb("p2", [Q, C])
        rp = sb("rp", [Q, C])
        a1 = sb("a1", [Q, C])
        a2 = sb("a2", [Q, C])
        nn = sb("nn", [Q, C])
        sc = sb("sc", [Q, C])
        ll = sb("ll", [Q, 2 * C])
        i64 = sb("i64", [Q, C])
        vv = sb("vv", [Q, C])
        m64 = sb("m64", [Q, C])
        hb = [sb(f"hb{i}", [Q, CH + 1, 2 * C]) for i in range(2)]
        st = sb("st", [P, C], F16)
        ms = sb("ms", [P, C], F16)
        kb = sb("kb", [Q, C])

        G = [ps(f"G{i}", [P, CH, C]) for i in range(2)]
        TP = ps("TP", [P, 512])
        U = ps("U", [P, 512])
        FD = ps("FD", [P, 512])
        TG = ps("TG", [P, 4, P])

        with ExitStack() as c2:
            def sb2(name, shape, dt=F32):
                return c2.enter_context(nc.sbuf_tensor(name, shape, dt))
            nat = sb2("nat", [P, L, 4, P])
            rnat = sb2("rnat", [3 * Q, C, 4, Q])
            rcmb = sb2("rcmb", [3 * Q, C, 4, Q])
            bnat = sb2("bnat", [C, 4, Q])
            d_nat = sem("d_nat")
            d_rec = sem("d_rec")
            d_w = sem("d_w")
            z_nat = sem("z_nat")
            z_id = sem("z_id")
            z_sel = sem("z_sel")
            z_pe = sem("z_pe")
            z_ev = sem("z_ev")
            z_rc = sem("z_rc")
            z_hi = sem("z_hi")
            z_init = sem("z_init")
            z_me = sem("z_me")
            with nc.Block() as block:
                N_W = 0

                @block.sync
                def _(sp):
                    nonlocal N_W
                    sp.wait_ge(z_nat, 1)
                    n = 0
                    for g, name in enumerate(("wi", "wf", "wz", "wo")):
                        for h in range(H):
                            sp.dma_start(nat[h * Q:(h + 1) * Q, :, g, h * Q:(h + 1) * Q],
                                         w[name][:, h, :, :].rearrange("l o d -> o l d")).then_inc(d_nat, 16)
                    for c in range(3):
                        sp.dma_start(rnat[c * Q:(c + 1) * Q, :, :, :],
                                     w["rker"].rearrange("l h d g o -> d (l h) g o")).then_inc(d_rec, 16)
                    loads = [
                        (up_w[:, :, :], w["ff_up"].rearrange("l d u -> d l u")),
                        (dn_w0[:, :, :], w["ff_down"][:, 0:P, :].rearrange("l u d -> u l d")),
                        (dn_w1[:, :, :], w["ff_down"][:, P:UP, :].rearrange("l u d -> u l d")),
                        (conv_w[:, :, :], w["conv_w"].rearrange("l d k -> d l k")),
                        (conv_b[:, :], w["conv_b"].rearrange("l d -> d l")),
                        (ln1_w[:, :], w["ln1_w"].rearrange("l d -> d l")),
                        (ln2_w[:, :], w["ln2_w"].rearrange("l d -> d l")),
                        (bnat[:, :, :], w["cell_b"].rearrange("l h g o -> (l h) g o")),
                        (scratch_in[0:S, :], x),
                        (scratch_in[S:(ITERS + 2) * CH, :], x[0:(ITERS + 2) * CH - S, :]),
                        (xin[0][0:Q, :], x[0:CH, :]),
                        (xin[1][0:Q, :], x[CH:2 * CH, :]),
                    ]
                    loads += [(gn_w[l * CH:(l + 1) * CH, :], w["gn_w"][l:l + 1, :].broadcast_to([CH, D])) for l in range(L)]
                    for dst, src in loads:
                        sp.dma_start(dst, src, allow_slow_non_contiguous=True).then_inc(d_w, 16)
                    sp.wait_ge(d_w, 16 * len(loads))

                @block.gpsimd
                def _(pool):
                    pool.memset(nat[:, :, :, :], 0.0).then_inc(z_nat, 1)
                    pool.memset(ident[:, :], 0.0).then_inc(z_id, 1)
                    pool.memset(pick[:, :, :], 0.0).then_inc(z_id, 1)
                    pool.wait_ge(z_id, 2)
                    pool.affine_select(out=ident[:, :], in_=ident[:, :], compare_op=ALU.not_equal, fill=1.0,
                                       base=0, pattern=[[-1, P]], channel_multiplier=1).then_inc(z_sel, 1)
                    pool.affine_select(out=pick[:, :, :], in_=pick[:, :, :], compare_op=ALU.not_equal, fill=1.0,
                                       base=0, pattern=[[0, CH], [-1, C]], channel_multiplier=1).then_inc(z_sel, 1)

                @block.tensor
                def _(pe):
                    pe.wait_ge(d_nat, 16 * 4 * H)
                    pe.wait_ge(z_sel, 1)
                    for l in range(L):
                        if l:
                            pe.wait_ge(z_ev, l)
                        for g in range(4):
                            last = pe.transpose(TG[:, g, :], nat[:, l, g, :], ident[:, :])
                        last.then_inc(z_pe, 1)

                @block.vector
                def _(dve):
                    v = nc.vector
                    v.memset(gate_b[:, :, :], 0.0).then_inc(z_init, 1)
                    v.memset(keep[:, :, :], 1.0).then_inc(z_init, 1)
                    v.memset(eps_ln[:, :], EPS)
                    v.memset(eps_gn[:, :], EPS * H_SCALE * H_SCALE)
                    v.memset(xn[:, :, :], 0.0)
                    v.memset(ad[:, :], 1.0)
                    v.memset(hb[0][:, :, :], 0.0)
                    v.memset(hb[1][:, :, :], 0.0)
                    v.memset(st[:, :], 0.0)
                    v.memset(ms[:, :], 0.0)
                    v.memset(m64[:, :], 0.0)
                    for q in range(1, L):
                        v.memset(xin[0][q * Q:(q + 1) * Q, :], 0.0)
                        v.memset(xin[1][q * Q:(q + 1) * Q, :], 0.0)
                    v.memset(m_eye[:, :], 0.0).then_inc(z_init, 1)
                    v.memset(rec_w[:, :, :], 0.0).then_inc(z_init, 1)
                    dve.wait_ge(z_init, 4)
                    for l in range(L):
                        v.memset(keep[:, LAG * l, l * H:(l + 1) * H], 0.0)
                    dve.wait_ge(z_sel, 1)
                    for q in range(2):
                        for g in range(2):
                            v.tensor_scalar(m_eye[q * Q:(q + 1) * Q, g * Q:(g + 1) * Q],
                                            ident[q * Q:(q + 1) * Q, q * Q:(q + 1) * Q],
                                            -G_SCALE / M_SCALE, None, ALU.mult)
                    for l in range(L):
                        dve.wait_ge(z_pe, l + 1)

                        def tg(g):
                            return TG[:, g, :].rearrange("p (h o) -> p h o", h=H)
                        v.tensor_scalar(gate_w[:, l, :, 0, :], tg(0), G_SCALE, None, ALU.mult).then_inc(z_me, 1)
                        v.tensor_scalar(gate_w[:, l, :, 2, :], tg(2), 2.0 * G_SCALE, None, ALU.mult)
                        v.tensor_scalar(gate_w[:, l, :, 3, :], tg(3), -G_SCALE, None, ALU.mult)
                        dve.wait_ge(z_me, l + 1)
                        v.scalar_tensor_tensor(out=gate_w[:, l, :, 1, :], in0=tg(1), scalar=-G_SCALE,
                                               in1=gate_w[:, l, :, 0, :], op0=ALU.mult, op1=ALU.add).then_inc(z_ev, 1)
                    dve.wait_ge(d_rec, 48)
                    cr = R_SCALE
                    v.tensor_scalar(rcmb[:, :, 0, :], rnat[:, :, 0, :], cr, None, ALU.mult).then_inc(z_rc, 1)
                    v.tensor_scalar(rcmb[:, :, 2, :], rnat[:, :, 2, :], 2.0 * cr, None, ALU.mult)
                    v.tensor_scalar(rcmb[:, :, 3, :], rnat[:, :, 3, :], -cr, None, ALU.mult)
                    dve.wait_ge(z_rc, 1)
                    v.scalar_tensor_tensor(out=rcmb[:, :, 1, :], in0=rnat[:, :, 1, :], scalar=-cr,
                                           in1=rcmb[:, :, 0, :], op0=ALU.mult, op1=ALU.add).then_inc(z_rc, 1)
                    dve.wait_ge(z_rc, 2)
                    v.tensor_copy(rec_w[0:3 * Q, :, :], rcmb[:, :, :, :].rearrange("p c g o -> p c (g o)")).then_inc(z_hi, 1)
                    dve.wait_ge(z_hi, 1)
                    v.tensor_tensor(rec_w[2 * Q:3 * Q, :, :],
                                    rcmb[2 * Q:3 * Q, :, :, :].rearrange("p c g o -> p c (g o)"),
                                    rec_w[2 * Q:3 * Q, :, :], ALU.subtract)
                    dve.wait_ge(d_w, 16 * (12 + L))
                    v.tensor_scalar(gate_b[0:C, 0, :], bnat[:, 0, :], G_SCALE, None, ALU.mult).then_inc(z_rc, 1)
                    v.tensor_scalar(gate_b[0:C, 2, :], bnat[:, 2, :], 2.0 * G_SCALE, None, ALU.mult)
                    v.tensor_scalar(gate_b[0:C, 3, :], bnat[:, 3, :], -G_SCALE, None, ALU.mult)
                    dve.wait_ge(z_rc, 3)
                    v.scalar_tensor_tensor(out=gate_b[0:C, 1, :], in0=bnat[:, 1, :], scalar=-G_SCALE,
                                           in1=gate_b[0:C, 0, :], op0=ALU.mult, op1=ALU.add)

        pre_ready, b_ready, gates_ready, bc_ready, t_ready = (
            sem(n) for n in ("pre_ready", "b_ready", "gates_ready", "bc_ready", "t_ready"))
        p1_ready, a1_ready, p2_ready, a2_ready, n_ready, r_ready = (
            sem(n) for n in ("p1_ready", "a1_ready", "p2_ready", "a2_ready", "n_ready", "r_ready"))
        h_ready, y_ready, h_split = (sem(n) for n in ("h_ready", "y_ready", "h_split"))
        s_clamped, ln_ready, v_ready, m_ready, m_split = (
            sem(n) for n in ("s_clamped", "ln_ready", "v_ready", "m_ready", "m_split"))
        B = {n: sem(n) for n in (
            "st1 mv1 ln1 rs1 nm1 tp1 hist xn1 tap add1 add2 cvb sge sg1 srr xcr gates_in "
            "yt ysum ymean yc ysq yvar gln grs gnm gnw x1r st2 mv2 ln2 rs2 nm2 tp2 n2r upr glr acr tpa atr dnr x2r ini mks"
        ).split()}
        d_xin, d_out = sem("d_xin"), sem("d_out")

        def bc(ap, n):
            return ap.unsqueeze(2).broadcast_to([*ap.shape, n])

        def by_layer(ap):
            return ap.rearrange("p (l t) -> p l t", l=L)

        def keep_at(parts, c):
            return keep[parts, bass.ds(c, 1), :].rearrange("p a c -> p (a c)")

        def norm_scale(a, var, n, scale, eps, var_ready, ln_done, rs_done, k):
            a.wait_ge(var_ready, k)
            nc.scalar.activation(lnv[:, 0:n], var, ACT.Ln, bias=eps[:, 0:1], scale=scale).then_inc(ln_done, 1)
            a.wait_ge(ln_done, k)
            nc.scalar.activation(rstd[:, 0:n], lnv[:, 0:n], ACT.Exp, scale=-0.5).then_inc(rs_done, 1)

        def dve_stats(dve, src, st_done, mv_done, k):
            nc.vector.bn_stats(stats[:, :], src).then_inc(st_done, 1)
            dve.wait_ge(st_done, k)
            nc.vector.bn_aggr(mv[:, :], stats[:, :]).then_inc(mv_done, 1)

        def dve_norm(dve, src, mv_done, rs_done, nm_done, k):
            dve.wait_ge(mv_done, k)
            dve.wait_ge(rs_done, k)
            nc.vector.tensor_scalar(normed[:, :], src, mv[:, 0:1], rstd[:, 0:1],
                                    ALU.subtract, ALU.mult).then_inc(nm_done, 1)

        def dve_xn(dve, k):
            dve.wait_ge(B["tp1"], k)
            dve.wait_ge(B["hist"], k)
            nc.vector.tensor_tensor(xn[:, :, K - 1:K - 1 + CH], by_layer(TP[:, 0:P]),
                                    bc(ln1_w[:, :], CH), ALU.mult).then_inc(B["xn1"], 1)

        def pool_history(pool, c):
            nc.gpsimd.tensor_tensor(xn[:, :, 0:K - 1], xn[:, :, CH:CH + K - 1],
                                    bc(keep[:, bass.ds(c, 1), 0:C:H].rearrange("p a l -> p (a l)"), K - 1),
                                    ALU.mult).then_inc(B["hist"], 1)

        def pool_conv(pool, k):
            pool.wait_ge(B["xn1"], k)
            for j in range(K):
                nc.gpsimd.tensor_tensor(taps[:, j, :, :], xn[:, :, j:j + CH], bc(conv_w[:, :, j], CH),
                                        ALU.mult).then_inc(B["tap"], 1)
            pool.wait_ge(B["tap"], K * (k - 1) + 2)
            nc.gpsimd.tensor_tensor(cv[:, :, :], taps[:, 0, :, :], taps[:, 1, :, :], ALU.add).then_inc(B["add1"], 1)
            pool.wait_ge(B["tap"], K * k)
            nc.gpsimd.tensor_tensor(cv2[:, :, :], taps[:, 2, :, :], taps[:, 3, :, :], ALU.add).then_inc(B["add1"], 1)
            pool.wait_ge(B["add1"], 2 * k)
            nc.gpsimd.tensor_tensor(cv[:, :, :], cv[:, :, :], cv2[:, :, :], ALU.add).then_inc(B["add2"], 1)
            pool.wait_ge(B["add2"], k)
            nc.gpsimd.tensor_tensor(cv2[:, :, :], cv[:, :, :], bc(conv_b[:, :], CH), ALU.add).then_inc(B["cvb"], 1)
            pool.wait_ge(B["sge"], k)
            nc.gpsimd.tensor_scalar(sg1[:, :, :], sg[:, :, :], 1.0, None, ALU.add).then_inc(B["sg1"], 1)

        def act_silu(a, k):
            a.wait_ge(B["cvb"], k)
            nc.scalar.activation(sg[:, :, :], cv2[:, :, :], ACT.Exp, scale=-1.0).then_inc(B["sge"], 1)

        def dve_silu(dve, k, half):
            dve.wait_ge(B["sg1"], k)
            a, b = half * L // 2, (half + 1) * L // 2
            nc.vector.reciprocal(sr[:, a:b, :], sg1[:, a:b, :]).then_inc(B["srr"], 1)

        def pool_silu(pool, k):
            pool.wait_ge(B["srr"], 2 * k)
            nc.gpsimd.tensor_tensor(xc[:, :, :], cv2[:, :, :], sr[:, :, :], ALU.mult).then_inc(B["xcr"], 1)

        def pe_norm_t(pe, nm_done, tp_done, k):
            pe.wait_ge(nm_done, k)
            pe.transpose(TP[:, 0:P], normed[:, :], ident[:, :]).then_inc(tp_done, 1)

        def pe_gate_bias(pe, g):
            pe.matmul(g[:, :, :].rearrange("p t c -> p (t c)"), gate_b[:, :, :].rearrange("p g o -> p (g o)"),
                      pick[:, :, :].rearrange("p t c -> p (t c)"), start=True, stop=False, skip_group_check=True)

        def pe_gates(pe, g, k, l, conv):
            pe.wait_ge(B["xcr"] if conv else B["xn1"], k)
            g0 = 0 if conv else 2
            for h in range(H):
                rhs = xc[:, l, :] if conv else xn[:, l, K - 1:K - 1 + CH]
                mm = pe.matmul(g[g0 * Q:(g0 + 2) * Q, :, l * H + h],
                               gate_w[:, l, h, g0:g0 + 2, :].rearrange("p g o -> p (g o)"),
                               rhs, start=False, stop=False, skip_group_check=True)
            return mm

        def dve_heads(dve, old):
            for l in range(L):
                ins = nc.vector.transpose(yt[l * CH:(l + 1) * CH, :, :],
                                          old[:, 1:CH + 1, l * H:(l + 1) * H].rearrange("p t h -> p h t"))
            ins.then_inc(B["yt"], 1)

        def dve_head_sum(dve, k):
            dve.wait_ge(B["yt"], k)
            nc.vector.tensor_reduce(ysum[:, :], yt[:, :, :], AX_X, ALU.add).then_inc(B["ysum"], 1)

        def dve_head_var(dve, k):
            dve.wait_ge(B["ysq"], k)
            nc.vector.tensor_reduce(yvar[:, :], ysq[:, :, :], AX_X, ALU.add).then_inc(B["yvar"], 1)

        def pool_heads(pool, residual, k):
            pl = nc.gpsimd
            pool.wait_ge(B["ysum"], k)
            pl.tensor_scalar(ysum[:, :], ysum[:, :], -1.0 / DH, None, ALU.mult).then_inc(B["ymean"], 1)
            pool.wait_ge(B["ymean"], k)
            pl.tensor_tensor(yc[:, :, :], yt[:, :, :], bc(ysum[:, :], DH), ALU.add).then_inc(B["yc"], 1)
            pool.wait_ge(B["yc"], k)
            pl.tensor_tensor(ysq[:, :, :], yc[:, :, :], yc[:, :, :], ALU.mult).then_inc(B["ysq"], 1)
            pool.wait_ge(B["grs"], k)
            pl.tensor_tensor(yt[:, :, :], yc[:, :, :], bc(rstd[:, :], DH), ALU.mult).then_inc(B["gnm"], 1)
            pool.wait_ge(B["gnm"], k)
            pl.tensor_tensor(yg[:, :], yt[:, :, :].rearrange("p h o -> p (h o)"), gn_w[:, :],
                             ALU.mult).then_inc(B["gnw"], 1)
            pool.wait_ge(B["gnw"], k)
            pl.tensor_tensor(x1[:, :], residual, yg[:, :], ALU.add).then_inc(B["x1r"], 1)

        def act_gelu(a, k):
            a.wait_ge(B["upr"], k)
            nc.scalar.activation(gl[:, :], U[:, 0:UP], ACT.Gelu).then_inc(B["glr"], 1)
            nc.scalar.preload_act_table_set("natural_log_exp_and_others")

        def dve_n2(dve, k):
            dve.wait_ge(B["tp2"], k)
            nc.vector.tensor_tensor(n2t[:, :, :], by_layer(TP[:, 0:P]), bc(ln2_w[:, :], CH),
                                    ALU.mult).then_inc(B["n2r"], 1)

        def dve_gated(dve, k):
            dve.wait_ge(B["glr"], k)
            nc.vector.tensor_tensor(act[:, :], U[:, UP:2 * UP], gl[:, :], ALU.mult).then_inc(B["acr"], 1)

        def dve_gated_t(dve, k):
            dve.wait_ge(B["tpa"], k)
            nc.vector.tensor_copy(at0[:, :], TP[:, 0:P])
            nc.vector.tensor_copy(at1[:, :], TP[0:UP - P, P:2 * P]).then_inc(B["atr"], 1)

        def dve_out(dve, k):
            dve.wait_ge(B["dnr"], k)
            nc.vector.tensor_tensor(x2[:, :], FD[:, 0:D], x1[:, :], ALU.add).then_inc(B["x2r"], 1)

        def pe_up(pe, k, layers):
            pe.wait_ge(B["n2r"], k)
            for l in layers:
                mm = pe.matmul(U[l * CH:(l + 1) * CH, 0:2 * UP], n2t[:, l, :], up_w[:, l, :], start=True, stop=True)
            return mm

        def pe_gated_t(pe, k):
            pe.wait_ge(B["acr"], k)
            pe.transpose(TP[:, 0:P], act[:, 0:P], ident[:, :])
            pe.transpose(TP[0:UP - P, P:2 * P], act[:, P:UP], ident[:, :]).then_inc(B["tpa"], 1)

        def pe_down(pe, k, layers):
            pe.wait_ge(B["atr"], k)
            for l in layers:
                pe.matmul(FD[l * CH:(l + 1) * CH, 0:D], at0[:, l * CH:(l + 1) * CH], dn_w0[:, l, :],
                          start=True, stop=False)
                mm = pe.matmul(FD[l * CH:(l + 1) * CH, 0:D], at1[:, l * CH:(l + 1) * CH], dn_w1[:, l, :],
                               start=False, stop=True)
            return mm

        with nc.Block() as block:
            @block.gpsimd
            def _(pool):
                pool_history(pool, 0)
                pool_conv(pool, 1)
                pool_silu(pool, 1)

            @block.scalar
            def _(a):
                nc.scalar.preload_act_table_set("natural_log_exp_and_others")
                norm_scale(a, mv[:, 1:2], 1, 1.0, eps_ln, B["mv1"], B["ln1"], B["rs1"], 1)
                act_silu(a, 1)

            @block.vector
            def _(dve):
                dve_stats(dve, xin[0][:, :], B["st1"], B["mv1"], 1)
                dve_norm(dve, xin[0][:, :], B["mv1"], B["rs1"], B["nm1"], 1)
                dve_xn(dve, 1)
                dve_silu(dve, 1, 0)
                dve_silu(dve, 1, 1)

            @block.tensor
            def _(pe):
                pe_norm_t(pe, B["nm1"], B["tp1"], 1)
                pe_gate_bias(pe, G[0])
                for conv in (False, True):
                    for l in range(L):
                        pe_gates(pe, G[0], 1, l, conv)

        nums = sorted(s.num for s in sems)
        assert nums == list(range(nums[0], nums[0] + len(nums)))
        nc.gpsimd.sem_clear(range(nums[0], nums[0] + len(nums)))
        nc.all_engine_barrier()

        with nc.Fori(0, ITERS // 2) as it:
            with nc.Block() as block:
                @block.sync
                def _(sp):
                    for p in range(2):
                        new = xin[(p + 1) % 2]
                        sp.wait_ge(B["x2r"], p + 1)
                        sp.dma_start(new[Q:P, :], x2[0:P - Q, :]).then_inc(d_xin, 16)
                        sp.dma_start(scratch_out[bass.ds(it * (2 * CH) + p * CH, CH), :], x2[P - Q:P, :]).then_inc(d_out, 16)
                        sp.dma_start(new[0:Q, :], scratch_in[bass.ds(it * (2 * CH) + (p + 1) * CH, CH), :]).then_inc(d_xin, 16)
                    sp.wait_ge(d_xin, 64)
                    sp.wait_ge(d_out, 32)

                @block.gpsimd
                def _(pool):
                    for p in range(2):
                        k = p + 1
                        pool_heads(pool, xin[(p + 1) % 2][:, :], k)
                        pool_history(pool, it * 2 + (p + 1))
                        pool_conv(pool, k)
                        pool_silu(pool, k)

                @block.scalar
                def _(a):
                    s = nc.scalar

                    def beside(t, k):
                        if t == 3:
                            norm_scale(a, yvar[:, :], H, 1.0 / DH, eps_gn, B["yvar"], B["gln"], B["grs"], k)
                        if t == 6:
                            norm_scale(a, mv[:, 1:2], 1, 1.0, eps_ln, B["mv2"], B["ln2"], B["rs2"], k)
                        if t == 10:
                            act_gelu(a, k)
                        if t == 16:
                            norm_scale(a, mv[:, 1:2], 1, 1.0, eps_ln, B["mv1"], B["ln1"], B["rs1"], k)
                        if t == 21:
                            act_silu(a, k)

                    for p in range(2):
                        g = G[p]
                        for t in range(CH):
                            n = p * CH + t + 1
                            a.wait_ge(pre_ready, n)
                            s.activation(eb[:, :], g[Q:2 * Q, t, :], ACT.Exp, scale=1.0 / G_SCALE).then_inc(b_ready, 1)
                            s.activation(ex[:, 0:C], g[0:Q, t, :], ACT.Exp, scale=1.0 / G_SCALE)
                            s.activation(ex[:, C:2 * C], g[2 * Q:3 * Q, t, :], ACT.Exp, scale=1.0 / G_SCALE)
                            s.activation(ex[:, 2 * C:3 * C], g[3 * Q:P, t, :], ACT.Exp,
                                         scale=1.0 / G_SCALE).then_inc(gates_ready, 1)
                            a.wait_ge(s_clamped, n)
                            s.activation(ll[:, 0:C], sc[:, :], ACT.Ln)
                            s.activation(ll[:, C:2 * C], sc[:, :], ACT.Ln, bias=1.0).then_inc(ln_ready, 1)
                            beside(t, p + 1)

                @block.tensor
                def _(pe):
                    def beside(t, p, k):
                        if t == 7:
                            pe_norm_t(pe, B["nm2"], B["tp2"], k)
                        if t in (8, 9):
                            mm = pe_up(pe, k, range((t - 8) * 2, (t - 8) * 2 + 2))
                            if t == 9:
                                mm.then_inc(B["upr"], 1)
                        if t == 11:
                            pe_gated_t(pe, k)
                        if t in (12, 13):
                            mm = pe_down(pe, k, range((t - 12) * 2, (t - 12) * 2 + 2))
                            if t == 13:
                                mm.then_inc(B["dnr"], 1)
                        if t == 14:
                            pe_gate_bias(pe, G[(p + 1) % 2])
                        if t == 17:
                            pe_norm_t(pe, B["nm1"], B["tp1"], k)
                        if 19 <= t < 19 + L:
                            pe_gates(pe, G[(p + 1) % 2], k, t - 19, False)
                        if 26 <= t < 26 + L:
                            pe_gates(pe, G[(p + 1) % 2], k, t - 26, True)

                    for p in range(2):
                        g = G[p]
                        for t in range(CH):
                            n = p * CH + t
                            if t == 0:
                                pe.wait_ge(B["ini"], p + 1)
                            else:
                                pe.wait_ge(h_split, n)
                            for c in range(C):
                                pe.matmul(g[:, t, c:c + 1], rec_w[:, c, :], st[:, c:c + 1],
                                          start=False, stop=False, skip_group_check=True)
                            if t:
                                pe.wait_ge(m_split, n)
                            pe.matmul(g[:, t, :], m_eye[:, :], ms[:, :],
                                      start=False, stop=True, skip_group_check=True).then_inc(pre_ready, 1)
                            beside(t, p, p + 1)

                @block.vector
                def _(dve):
                    v = nc.vector

                    def beside(t, p, k):
                        old = hb[(p + 1) % 2]
                        if t == 0:
                            dve_heads(dve, old)
                        if t == 1:
                            dve_head_sum(dve, k)
                        if t == 2:
                            dve_head_var(dve, k)
                        if t == 5:
                            dve.wait_ge(B["x1r"], k)
                            dve_stats(dve, x1[:, :], B["st2"], B["mv2"], k)
                        if t == 6:
                            dve_norm(dve, x1[:, :], B["mv2"], B["rs2"], B["nm2"], k)
                        if t == 7:
                            dve_n2(dve, k)
                        if t == 10:
                            dve_gated(dve, k)
                        if t == 11:
                            dve_gated_t(dve, k)
                        if t == 13:
                            dve_out(dve, k)
                        new = xin[(p + 1) % 2]
                        if t == 15:
                            dve.wait_ge(d_xin, 32 * k)
                            dve_stats(dve, new[:, :], B["st1"], B["mv1"], k)
                        if t == 16:
                            dve_norm(dve, new[:, :], B["mv1"], B["rs1"], B["nm1"], k)
                        if t == 17:
                            dve_xn(dve, k)
                        if t in (22, 23):
                            dve_silu(dve, k, t - 22)

                    for p in range(2):
                        c = it * 2 + p
                        m0 = 5 * p
                        if p:
                            dve.wait_ge(m_ready, CH)
                            dve.wait_ge(y_ready, CH)
                        v.tensor_tensor(m64[:, :], m64[:, :], keep_at(slice(0, Q), c), ALU.mult).then_inc(B["mks"], 1)
                        v.tensor_scalar(kb[:, :], keep_at(slice(0, Q), c), 1.0, -M_START * M_SCALE,
                                        ALU.subtract, ALU.mult).then_inc(B["mks"], 1)
                        v.tensor_tensor(hb[p][:, 0, C:2 * C], hb[1 - p][:, CH, C:2 * C], keep_at(slice(0, Q), c),
                                        ALU.mult)
                        if p:
                            dve.wait_ge(h_split, CH)
                        v.tensor_tensor(st[0:3 * Q, :], st[0:3 * Q, :], keep_at(slice(0, 3 * Q), c),
                                        ALU.mult).then_inc(B["mks"], 1)
                        dve.wait_ge(B["mks"], m0 + 3)
                        v.tensor_tensor(m64[:, :], m64[:, :], kb[:, :], ALU.add).then_inc(B["mks"], 1)
                        dve.wait_ge(B["mks"], m0 + 4)
                        v.tensor_copy(ms[0:Q, :], m64[:, :]).then_inc(B["mks"], 1)
                        dve.wait_ge(B["mks"], m0 + 5)
                        v.tensor_tensor(ms[Q:2 * Q, :], m64[:, :], ms[0:Q, :], ALU.subtract).then_inc(B["ini"], 1)

                        g, now = G[p], hb[p]
                        for t in range(CH):
                            n = p * CH + t + 1
                            dve.wait_ge(b_ready, n)
                            v.tensor_scalar(ad[:, 0:C], eb[:, :], E_TOP, None, ALU.min).then_inc(bc_ready, 1)
                            dve.wait_ge(bc_ready, n)
                            dve.wait_ge(gates_ready, n)
                            v.scalar_tensor_tensor(out=tt[:, :], in0=ex[:, :], scalar=E_TOP, in1=ad[:, :],
                                                   op0=ALU.min, op1=ALU.add).then_inc(t_ready, 1)
                            s_, z1, o1 = tt[:, 0:C], tt[:, C:2 * C], tt[:, 2 * C:3 * C]
                            dve.wait_ge(t_ready, n)
                            v.scalar_tensor_tensor(out=p1[:, :], in0=s_, scalar=1.0, in1=z1,
                                                   op0=ALU.add, op1=ALU.mult).then_inc(p1_ready, 1)
                            v.tensor_tensor(a1[:, :], now[:, t, C:2 * C], s_, ALU.add).then_inc(a1_ready, 1)
                            v.tensor_scalar(sc[:, :], s_, LN_LOW, None, ALU.max).then_inc(s_clamped, 1)
                            dve.wait_ge(p1_ready, n)
                            v.tensor_tensor(p2[:, :], p1[:, :], o1, ALU.mult).then_inc(p2_ready, 1)
                            dve.wait_ge(a1_ready, n)
                            v.tensor_tensor(a2[:, :], a1[:, :], z1, ALU.mult).then_inc(a2_ready, 1)
                            dve.wait_ge(p2_ready, n)
                            v.reciprocal(rp[:, :], p2[:, :]).then_inc(r_ready, 1)
                            dve.wait_ge(a2_ready, n)
                            v.scalar_tensor_tensor(out=nn[:, :], in0=s_, scalar=-2.0, in1=a2[:, :],
                                                   op0=ALU.mult, op1=ALU.add).then_inc(n_ready, 1)
                            v.scalar_tensor_tensor(out=i64[:, :], in0=g[0:Q, t, :], scalar=M_SCALE / G_SCALE,
                                                   in1=m64[:, :], op0=ALU.mult, op1=ALU.add)
                            dve.wait_ge(n_ready, n)
                            v.scalar_tensor_tensor(out=st[0:Q, :], in0=nn[:, :], scalar=H_SCALE, in1=rp[:, :],
                                                   op0=ALU.mult, op1=ALU.mult)
                            v.scalar_tensor_tensor(out=now[:, t + 1, 0:C], in0=nn[:, :], scalar=H_SCALE, in1=rp[:, :],
                                                   op0=ALU.mult, op1=ALU.mult).then_inc(h_ready, 1)
                            v.scalar_tensor_tensor(out=st[2 * Q:3 * Q, :], in0=nn[:, :], scalar=H_SCALE, in1=rp[:, :],
                                                   op0=ALU.mult, op1=ALU.mult)
                            dve.wait_ge(h_ready, n)
                            v.tensor_tensor(st[Q:2 * Q, :], now[:, t + 1, 0:C], st[0:Q, :],
                                            ALU.subtract).then_inc(h_split, 1)
                            dve.wait_ge(ln_ready, n)
                            v.tensor_tensor(vv[:, :], ll[:, C:2 * C], ll[:, 0:C], ALU.subtract).then_inc(v_ready, 1)
                            v.scalar_tensor_tensor(out=now[:, t + 1, C:2 * C], in0=now[:, t + 1, 0:C],
                                                   scalar=1.0 / H_SCALE, in1=o1, op0=ALU.mult,
                                                   op1=ALU.mult).then_inc(y_ready, 1)
                            dve.wait_ge(v_ready, n)
                            v.scalar_tensor_tensor(out=ms[0:Q, :], in0=vv[:, :], scalar=M_SCALE, in1=i64[:, :],
                                                   op0=ALU.mult, op1=ALU.add)
                            v.scalar_tensor_tensor(out=m64[:, :], in0=vv[:, :], scalar=M_SCALE, in1=i64[:, :],
                                                   op0=ALU.mult, op1=ALU.add).then_inc(m_ready, 1)
                            dve.wait_ge(m_ready, n)
                            v.tensor_tensor(ms[Q:2 * Q, :], m64[:, :], ms[0:Q, :], ALU.subtract).then_inc(m_split, 1)
                            beside(t, p, p + 1)

            nc.gpsimd.sem_clear(range(nums[0], nums[0] + len(nums)))
            nc.all_engine_barrier()

        with nc.Block() as block:
            @block.sync
            def _(sp):
                sp.wait_ge(B["x2r"], 1)
                sp.dma_start(scratch_out[ITERS * CH:(ITERS + 1) * CH, :], x2[P - Q:P, :]).then_inc(d_out, 16)
                sp.wait_ge(d_out, 16)

            @block.gpsimd
            def _(pool):
                pool_heads(pool, xin[(ITERS - 1) % 2][:, :], 1)

            @block.scalar
            def _(a):
                norm_scale(a, yvar[:, :], H, 1.0 / DH, eps_gn, B["yvar"], B["gln"], B["grs"], 1)
                norm_scale(a, mv[:, 1:2], 1, 1.0, eps_ln, B["mv2"], B["ln2"], B["rs2"], 1)
                act_gelu(a, 1)

            @block.tensor
            def _(pe):
                pe_norm_t(pe, B["nm2"], B["tp2"], 1)
                pe_up(pe, 1, range(L)).then_inc(B["upr"], 1)
                pe_gated_t(pe, 1)
                pe_down(pe, 1, range(L)).then_inc(B["dnr"], 1)

            @block.vector
            def _(dve):
                dve_heads(dve, hb[(ITERS - 1) % 2])
                dve_head_sum(dve, 1)
                dve_head_var(dve, 1)
                dve.wait_ge(B["x1r"], 1)
                dve_stats(dve, x1[:, :], B["st2"], B["mv2"], 1)
                dve_norm(dve, x1[:, :], B["mv2"], B["rs2"], B["nm2"], 1)
                dve_n2(dve, 1)
                dve_gated(dve, 1)
                dve_gated_t(dve, 1)
                dve_out(dve, 1)

        nc.gpsimd.sem_clear(range(nums[0], nums[0] + len(nums)))
        nc.all_engine_barrier()


def attention_stage(nc, x, ctx_in, w, scratch_out, first_row, att_out, xa_out, dims):
    S, D, HEADS, DHEAD, NK, DC = dims
    CH = Q
    NCH = S // CH
    TILES = S // P
    N = HEADS * CH
    KT = (NK + P - 1) // P
    LAST = NK - (KT - 1) * P
    GRP = N // P
    HPG = P // CH
    KC = [(i, min(i + 512, NK)) for i in range(0, NK, 512)]
    assert N == 512

    with ExitStack() as ctx:
        def sb(name, shape, dt=F32):
            return ctx.enter_context(nc.sbuf_tensor(name, shape, dt))

        sems = []

        def sem(name):
            s = ctx.enter_context(nc.semaphore(name))
            sems.append(s)
            return s

        def ps(name, shape, dt=F32):
            return ctx.enter_context(nc.psum_tensor(name, shape, dt))

        identa = sb("identa", [P, P])
        keys_t = sb("keys_t", [DC + 1, KT, P])
        keys_b = sb("keys_b", [DC, KT * P], BF16)
        vals = sb("vals", [P, KT, DC + 1])
        qk_w = sb("qk_w", [P, HEADS, DC])
        vo_w = sb("vo_w", [DC + 1, HEADS, D + 1])
        xat = sb("xat", [P, S])
        fold = sb("fold", [P, CH])
        neg_sel = sb("neg_sel", [P, DC + 1])
        wq_sb = sb("wq_sb", [P, HEADS * DHEAD])
        wk_sb = sb("wk_sb", [DC, HEADS * DHEAD])
        wv_sb = sb("wv_sb", [DC, HEADS * DHEAD])
        wo_sb = sb("wo_sb", [DHEAD, HEADS, D])
        wt = sb("wt", [DHEAD, 3, P])
        post_w = sb("post_w", [P, D])
        eps_a = sb("eps_a", [P, 1])
        xs = sb("xs", [P, TILES, D])
        xo = sb("xo", [P, TILES, D])
        sta = sb("sta", [P, TILES, 6])
        mva = sb("mva", [P, TILES, 2])
        rsa = sb("rsa", [P, TILES])
        q_f = sb("q_f", [DC + 1, N])
        q_b = sb("q_b", [DC, N], BF16)
        mx = sb("mx", [P, GRP, len(KC)])
        mxn = sb("mxn", [P, GRP])
        dg = sb("dg", [P, GRP, P])
        NP_ = 4
        pr = sb("pr", [P, NP_, N])
        o_sb = sb("o_sb", [DC + 1, N])
        rden = sb("rden", [P, GRP])
        yacc = sb("yacc", [P, GRP, D])
        ysb = sb("ysb", [CH, D])

        SP_ = [ps(f"SP{i}", [P, 512]) for i in range(4)]
        OP = ps("OP", [P, 512])
        QP = ps("QP", [P, 512])
        YP = [ps(f"YP{i}", [P, 512]) for i in range(2)]

        d_ctx, d_wt, d_x, d_y = (sem(n) for n in ("d_ctx", "d_wt", "d_x", "d_y"))
        c_zero, c_ident, w_t, w_tc, w_p, w_pc, k_t, k_tc = (
            sem(n) for n in ("c_zero", "c_ident", "w_t", "w_tc", "w_p", "w_pc", "k_t", "k_tc"))
        n_stat, n_mv, n_ln, n_rs, n_x, n_w, n_r, n_t, n_tc = (
            sem(n) for n in ("n_stat", "n_mv", "n_ln", "n_rs", "n_x", "n_w", "n_r", "n_t", "n_tc"))

        with nc.Block() as block:
            @block.sync
            def _(sp):
                sp.wait_ge(c_zero, 3)
                full = (KT - 1) * P
                sp.dma_start(vals[:, 0:KT - 1, 0:DC], ctx_in[0:full, :].rearrange("(j p) d -> p j d", p=P)).then_inc(d_ctx, 16)
                sp.dma_start(vals[0:LAST, KT - 1, 0:DC], ctx_in[full:NK, :]).then_inc(d_ctx, 16)
                for dst, src in ((wq_sb[:, :], w["Wq"]), (wk_sb[:, :], w["Wk"]), (wv_sb[:, :], w["Wv"]),
                                 (wo_sb[:, :, :], w["Wo"].rearrange("(h i) n -> i h n", i=DHEAD)),
                                 (post_w[:, :], w["post_w"].unsqueeze(0).broadcast_to([P, D]))):
                    sp.dma_start(dst, src).then_inc(d_wt, 16)
                sp.dma_start(xs[:, :, :], scratch_out[first_row:first_row + S, :].rearrange("(j p) d -> p j d", p=P)).then_inc(d_x, 16)
                sp.dma_start(xo[:, :, :], x.rearrange("(j p) d -> p j d", p=P)).then_inc(d_x, 16)
                sp.wait_ge(n_r, 2 * TILES)
                sp.dma_start(xa_out.rearrange("(j p) d -> p j d", p=P), xo[:, :, :]).then_inc(d_y, 16)
                sp.wait_ge(d_y, 16)

            @block.gpsimd
            def _(pool):
                pool.memset(vals[:, :, :], 0.0).then_inc(c_zero, 1)
                pool.memset(identa[:, :], 0.0).then_inc(c_zero, 1)
                pool.wait_ge(c_zero, 2)
                pool.memset(vals[:, :, DC:DC + 1], 1.0).then_inc(c_zero, 1)
                pool.affine_select(out=identa[:, :], in_=identa[:, :], compare_op=ALU.not_equal, fill=1.0,
                                   base=0, pattern=[[-1, P]], channel_multiplier=1).then_inc(c_ident, 1)
                pool.memset(neg_sel[:, :], 0.0).then_inc(c_ident, 1)
                pool.wait_ge(c_ident, 2)
                pool.memset(neg_sel[:, DC:DC + 1], -1.0).then_inc(c_ident, 1)

            @block.scalar
            def _(a):
                s = nc.scalar
                s.preload_act_table_set("natural_log_exp_and_others")
                for r in range(2):
                    for j in range(TILES):
                        a.wait_ge(n_mv, r * TILES + j + 1)
                        s.activation(rsa[:, j:j + 1], mva[:, j, 1:2], ACT.Ln, bias=eps_a[:, 0:1]).then_inc(n_ln, 1)
                        a.wait_ge(n_ln, r * TILES + j + 1)
                        s.activation(rsa[:, j:j + 1], rsa[:, j:j + 1], ACT.Exp, scale=-0.5).then_inc(n_rs, 1)

            @block.tensor
            def _(pe):
                pe.wait_ge(c_ident, 1)
                pe.wait_ge(d_wt, 16 * 5)
                for h in range(HEADS):
                    if h:
                        pe.wait_ge(w_tc, h)
                    cols = slice(h * DHEAD, (h + 1) * DHEAD)
                    pe.transpose(SP_[0][0:DHEAD, 0:P], wq_sb[:, cols], identa[:, :])
                    pe.transpose(SP_[0][0:DHEAD, P:P + DC], wk_sb[:, cols], identa[0:DC, 0:DC])
                    pe.transpose(SP_[0][0:DHEAD, 2 * P:2 * P + DC], wv_sb[:, cols], identa[0:DC, 0:DC]).then_inc(w_t, 1)
                    pe.wait_ge(w_tc, h + 1)
                    if h:
                        pe.wait_ge(w_pc, h)
                    pe.matmul(SP_[1][:, 0:DC], wt[:, 0, :], wt[:, 1, 0:DC], start=True, stop=True)
                    pe.matmul(SP_[1][0:DC, P:2 * P], wt[:, 2, 0:DC], wo_sb[:, h, :], start=True, stop=True).then_inc(w_p, 1)
                pe.wait_ge(d_ctx, 32)
                for j in range(0, KT, 4):
                    b = SP_[2 + (j // 4) % 2]
                    if j >= 8:
                        pe.wait_ge(k_tc, j // 4 - 1)
                    for i in range(j, min(j + 4, KT)):
                        mm = pe.transpose(b[0:DC, (i - j) * P:(i - j + 1) * P], vals[:, i, 0:DC], identa[:, :])
                    mm.then_inc(k_t, 1)
                for j in range(TILES):
                    pe.wait_ge(n_r, TILES + j + 1)
                    if j:
                        pe.wait_ge(n_tc, j)
                    pe.transpose(SP_[0][:, 0:P], xo[:, j, :], identa[:, :]).then_inc(n_t, 1)

            @block.vector
            def _(dve):
                v = nc.vector
                v.memset(eps_a[:, :], EPS)
                v.memset(vo_w[:, :, :], 0.0)
                v.memset(keys_t[:, :, :], 1.0).then_inc(n_w, 1)
                dve.wait_ge(n_w, 1)
                v.memset(vo_w[DC:DC + 1, :, D:D + 1], 1.0)
                dve.wait_ge(c_ident, 1)
                v.tensor_reduce(fold[:, :], identa[:, :].rearrange("p (h t) -> p t h", h=HPG), AX_X, ALU.add)
                for h in range(HEADS):
                    dve.wait_ge(w_t, h + 1)
                    v.tensor_copy(wt[:, 0, :], SP_[0][0:DHEAD, 0:P])
                    v.tensor_copy(wt[:, 1:3, 0:DC], SP_[0][0:DHEAD, P:3 * P].rearrange("p (a c) -> p a c", a=2)[:, :, 0:DC]).then_inc(w_tc, 1)
                    dve.wait_ge(w_p, h + 1)
                    v.tensor_scalar(qk_w[:, h, :], SP_[1][:, 0:DC], float(DHEAD) ** -0.5, None, ALU.mult)
                    v.tensor_copy(vo_w[0:DC, h, 0:D], SP_[1][0:DC, P:2 * P]).then_inc(w_pc, 1)
                for j in range(0, KT, 4):
                    b = SP_[2 + (j // 4) % 2]
                    n = min(4, KT - j)
                    dve.wait_ge(k_t, j // 4 + 1)
                    v.tensor_copy(keys_t[0:DC, j:j + n, :].rearrange("p a c -> p (a c)"), b[0:DC, 0:n * P])
                    v.tensor_copy(keys_b[:, j * P:(j + n) * P], b[0:DC, 0:n * P]).then_inc(k_tc, 1)
                dve.wait_ge(d_x, 32)
                dve.wait_ge(d_wt, 16 * 5)
                for r, buf in ((0, xs), (1, xo)):
                    if r:
                        dve.wait_ge(n_r, TILES)
                    for j in range(TILES):
                        k = r * TILES + j + 1
                        v.bn_stats(sta[:, j, :], buf[:, j, :]).then_inc(n_stat, 1)
                        dve.wait_ge(n_stat, k)
                        v.bn_aggr(mva[:, j, :], sta[:, j, :]).then_inc(n_mv, 1)
                    for j in range(TILES):
                        k = r * TILES + j + 1
                        dve.wait_ge(n_mv, k)
                        dve.wait_ge(n_rs, k)
                        v.tensor_scalar(buf[:, j, :], buf[:, j, :], mva[:, j, 0:1], rsa[:, j:j + 1],
                                        ALU.subtract, ALU.mult).then_inc(n_r if r else n_x, 1)
                        if r == 0:
                            dve.wait_ge(n_x, k)
                            v.tensor_tensor(xs[:, j, :], xs[:, j, :], post_w[:, :], ALU.mult).then_inc(n_w, 1)
                            dve.wait_ge(n_w, j + 2)
                            v.tensor_tensor(xo[:, j, :], xo[:, j, :], xs[:, j, :], ALU.add).then_inc(n_r, 1)
                            dve.wait_ge(n_r, j + 1)
                for j in range(TILES):
                    dve.wait_ge(n_t, j + 1)
                    v.tensor_copy(xat[:, j * P:(j + 1) * P], SP_[0][:, 0:P]).then_inc(n_tc, 1)

        q_done, q_copied, m_done, m_max, m_neg, dg_done, q_row, q_full = (
            sem(n) for n in ("q_done", "q_copied", "m_done", "m_max", "m_neg", "dg_done", "q_row", "q_full"))
        s_done, p_done, o_done, o_copied, y_done, rd_done, y_acc, y_fold, y_copied, y_out = (
            sem(n) for n in ("s_done", "p_done", "o_done", "o_copied", "y_done", "rd_done", "y_acc", "y_fold", "y_copied", "y_out"))
        nums = sorted(s.num for s in sems)
        assert nums == list(range(nums[0], nums[0] + len(nums)))
        nc.gpsimd.sem_clear(range(nums[0], nums[0] + len(nums)))
        nc.all_engine_barrier()
        with nc.Fori(0, NCH) as it:
            with nc.Block() as block:
                @block.sync
                def _(sp):
                    sp.wait_ge(y_copied, 1)
                    sp.dma_start(att_out[bass.ds(it * CH, CH), :], ysb[:, :]).then_inc(y_out, 16)
                    sp.wait_ge(y_out, 16)

                @block.scalar
                def _(a):
                    s = nc.scalar
                    for j in range(KT):
                        k = LAST if j == KT - 1 else P
                        a.wait_ge(s_done, j + 1)
                        if j >= NP_:
                            a.wait_ge(o_done, j - NP_ + 1)
                        s.activation(pr[0:k, j % NP_, :], SP_[j % 4][0:k, :], ACT.Exp).then_inc(p_done, 1)

                @block.tensor
                def _(pe):
                    for h in range(HEADS):
                        mm = pe.matmul(QP[0:DC, h * CH:(h + 1) * CH], qk_w[:, h, :], xat[:, bass.ds(it * CH, CH)],
                                       start=(h == 0), stop=True, skip_group_check=True)
                    mm.then_inc(q_done, 1)
                    pe.wait_ge(q_copied, 1)
                    n = 0
                    for g in range(GRP):
                        for a0, a1 in KC:
                            if n >= 4:
                                pe.wait_ge(m_max, n - 3)
                            pe.matmul(SP_[n % 4][:, 0:a1 - a0], q_b[:, g * P:(g + 1) * P], keys_b[:, a0:a1],
                                      start=True, stop=True).then_inc(m_done, 1)
                            n += 1
                    pe.wait_ge(dg_done, 1)
                    pe.matmul(OP[0:DC + 1, :], neg_sel[:, :], dg[:, :, :].rearrange("p g c -> p (g c)"),
                              start=True, stop=True).then_inc(q_row, 1)
                    pe.wait_ge(q_full, 1)
                    pe.wait_ge(m_max, n)

                    def scores(j):
                        k = LAST if j == KT - 1 else P
                        if j >= 4:
                            pe.wait_ge(p_done, j - 3)
                        pe.matmul(SP_[j % 4][0:k, :], keys_t[:, j, 0:k], q_f[:, :], start=True, stop=True).then_inc(s_done, 1)

                    scores(0)
                    scores(1)
                    for j in range(KT):
                        if j + 2 < KT:
                            scores(j + 2)
                        k = LAST if j == KT - 1 else P
                        pe.wait_ge(p_done, j + 1)
                        pe.matmul(OP[0:DC + 1, :], vals[0:k, j, :], pr[0:k, j % NP_, :],
                                  start=(j == 0), stop=(j == KT - 1)).then_inc(o_done, 1)
                    pe.wait_ge(o_copied, 1)
                    for h in range(HEADS):
                        r, gq = h % HPG, h // HPG
                        mm = pe.matmul(YP[gq // 2][r * CH:(r + 1) * CH, (gq % 2) * 256:(gq % 2) * 256 + D + 1],
                                       o_sb[:, h * CH:(h + 1) * CH], vo_w[:, h, :], start=True, stop=True)
                    mm.then_inc(y_done, 1)
                    pe.wait_ge(y_acc, GRP)
                    for gq in range(GRP):
                        mm = pe.matmul(QP[0:CH, 0:D], fold[:, :], yacc[:, gq, :], start=(gq == 0), stop=(gq == GRP - 1))
                    mm.then_inc(y_fold, 1)

                @block.vector
                def _(dve):
                    v = nc.vector
                    dve.wait_ge(q_done, 1)
                    v.tensor_copy(q_b[:, :], QP[0:DC, :]).then_inc(q_copied, 1)
                    v.tensor_copy(q_f[0:DC, :], QP[0:DC, :])
                    n = 0
                    for g in range(GRP):
                        for i, (a0, a1) in enumerate(KC):
                            dve.wait_ge(m_done, n + 1)
                            v.tensor_reduce(mx[:, g, i:i + 1], SP_[n % 4][:, 0:a1 - a0], AX_X, ALU.max).then_inc(m_max, 1)
                            n += 1
                    dve.wait_ge(m_max, n)
                    v.tensor_reduce(mxn[:, :], mx[:, :, :], AX_X, ALU.max).then_inc(m_neg, 1)
                    dve.wait_ge(m_neg, 1)
                    for g in range(GRP):
                        ins = v.tensor_scalar(dg[:, g, :], identa[:, :], mxn[:, g:g + 1], None, ALU.mult)
                    ins.then_inc(dg_done, 1)
                    dve.wait_ge(q_row, 1)
                    v.tensor_copy(q_f[DC:DC + 1, :], OP[DC:DC + 1, :]).then_inc(q_full, 1)
                    dve.wait_ge(o_done, KT)
                    v.tensor_copy(o_sb[:, :], OP[0:DC + 1, :]).then_inc(o_copied, 1)
                    dve.wait_ge(y_done, 1)
                    for gq in range(GRP):
                        y = YP[gq // 2][:, (gq % 2) * 256:(gq % 2) * 256 + D + 1]
                        ins = v.reciprocal(rden[:, gq:gq + 1], y[:, D:D + 1])
                    ins.then_inc(rd_done, 1)
                    dve.wait_ge(rd_done, 1)
                    for gq in range(GRP):
                        y = YP[gq // 2][:, (gq % 2) * 256:(gq % 2) * 256 + D + 1]
                        v.tensor_scalar(yacc[:, gq, :], y[:, 0:D], rden[:, gq:gq + 1], None, ALU.mult).then_inc(y_acc, 1)
                    dve.wait_ge(y_fold, 1)
                    v.tensor_copy(ysb[:, :], QP[0:CH, 0:D]).then_inc(y_copied, 1)

            nc.gpsimd.sem_clear(range(nums[0], nums[0] + len(nums)))
            nc.all_engine_barrier()


def experts_stage(nc, att, xa, w, bo, row_p, row_i, out, dims):
    S, D, E, FF, CAP = dims
    TILES = S // P
    FC = FF // P
    HALF = 512
    with ExitStack() as ctx:
        def sb(name, shape, dt=F32):
            return ctx.enter_context(nc.sbuf_tensor(name, shape, dt))

        def sem(name):
            return ctx.enter_context(nc.semaphore(name))

        def ps(name, shape, dt=F32):
            return ctx.enter_context(nc.psum_tensor(name, shape, dt))

        idente = sb("idente", [P, P])
        w1 = sb("w1", [P, E, FF])
        w2 = sb("w2", [P, E, FC, D])
        b1n = sb("b1n", [E * FC, P])
        b1t = sb("b1t", [P, E * FC])
        b2r = sb("b2r", [1, E, D])
        ones = sb("ones", [1, P])
        rwn = sb("rwn", [E, D])
        rwt = sb("rwt", [P, E])
        bo_r = sb("bo_r", [P, D])
        eps_e = sb("eps_e", [P, 1])
        xb = sb("xb", [P, TILES, D])
        ya = sb("ya", [P, TILES, D])
        xbt = sb("xbt", [P, S])
        lg = sb("lg", [P, TILES, E])
        le = sb("le", [P, TILES, E])
        lmax = sb("lmax", [P, TILES])
        lsum = sb("lsum", [P, TILES])
        prob = sb("prob", [P, TILES])
        cand = sb("cand", [P, TILES, E])
        weigh = sb("weigh", [P, E])
        idx = sb("idx", [P, TILES])
        prow = sb("prow", [P, S])
        irow = sb("irow", [P, S])
        before = sb("before", [P, 2 * S])
        beat = sb("beat", [P, S])
        tie = sb("tie", [P, S])
        rank = sb("rank", [P, TILES])
        kept = sb("kept", [P, TILES])
        fin_e = sb("fin_e", [P, TILES])
        mask = sb("mask", [P, TILES, E])
        hid = sb("hid", [P, 2, FC, S])
        acc = sb("acc", [P, TILES, D])
        st_e = sb("st_e", [P, TILES, 6])
        mv_e = sb("mv_e", [P, TILES, 2])
        rs_e = sb("rs_e", [P, TILES])
        HP = [ps(f"HP{i}", [P, 512]) for i in range(4)]
        YE = [ps(f"YE{i}", [P, 512]) for i in range(2)]
        TE = [ps(f"TE{i}", [P, 512]) for i in range(2)]

        e_w, e_w2, e_x, e_row, e_out, e_sc = (sem(n) for n in ("e_w", "e_w2", "e_x", "e_row", "e_out", "e_sc"))
        e_id, e_z, e_wg, e_bt, e_btc = (sem(n) for n in ("e_id", "e_z", "e_wg", "e_bt", "e_btc"))
        e_add, e_add2, e_st, e_mv, e_ln, e_rs, e_xb, e_t, e_tc, e_lg, e_lgc = (
            sem(n) for n in ("e_add", "e_add2", "e_st", "e_mv", "e_ln", "e_rs", "e_xb", "e_t", "e_tc", "e_lg", "e_lgc"))
        e_max, e_exp, e_sum, e_p, e_c, e_c2, e_i0, e_i, e_g, e_tie, e_b, e_rk, e_kp, e_fe, e_mk = (
            sem(n) for n in ("e_max", "e_exp", "e_sum", "e_p", "e_c", "e_c2", "e_i0", "e_i", "e_g", "e_tie", "e_b", "e_rk", "e_kp", "e_fe", "e_mk"))
        e_h, e_hr, e_y, e_ya, e_fin, e_st2, e_mv2, e_ln2, e_rs2 = (
            sem(n) for n in ("e_h", "e_hr", "e_y", "e_ya", "e_fin", "e_st2", "e_mv2", "e_ln2", "e_rs2"))
        NW = 4

        with nc.Block() as block:
            @block.sync
            def _(sp):
                sp.dma_start(xb[:, :, :], xa.rearrange("(j p) d -> p j d", p=P)).then_inc(e_x, 16)
                sp.dma_start(ya[:, :, :], att.rearrange("(j p) d -> p j d", p=P)).then_inc(e_x, 16)
                sp.dma_start(bo_r[:, :], bo.unsqueeze(0).broadcast_to([P, D])).then_inc(e_w, 16)
                sp.dma_start(rwn[:, :], w["router_w"]).then_inc(e_w, 16)
                sp.dma_start(b1n[:, :], w["b1"].rearrange("e (c p) -> (e c) p", p=P)).then_inc(e_w, 16)
                sp.dma_start(b2r[:, :, :], w["b2"].unsqueeze(0)).then_inc(e_w, 16)
                for e in range(E):
                    sp.dma_start(w1[:, e, :], w["W1"][e]).then_inc(e_w2, 16)
                    sp.dma_start(w2[:, e, :, :], w["W2"][e].rearrange("(c p) d -> p c d", p=P)).then_inc(e_w2, 16)
                sp.wait_ge(e_p, 1)
                sp.wait_ge(e_i, 1)
                sp.dma_start(row_p.rearrange("(j p) -> p j", p=P), prob[:, :], allow_slow_non_contiguous=True).then_inc(e_sc, 16)
                sp.dma_start(row_i.rearrange("(j p) -> p j", p=P), idx[:, :], allow_slow_non_contiguous=True).then_inc(e_sc, 16)
                sp.wait_ge(e_sc, 32)
                sp.dma_start(prow[:, :], row_p.unsqueeze(0).broadcast_to([P, S])).then_inc(e_row, 16)
                sp.dma_start(irow[:, :], row_i.unsqueeze(0).broadcast_to([P, S])).then_inc(e_row, 16)
                sp.wait_ge(e_fin, TILES)
                sp.dma_start(out.rearrange("(j p) d -> p j d", p=P), acc[:, :, :]).then_inc(e_out, 16)
                sp.wait_ge(e_out, 16)

            @block.gpsimd
            def _(pool):
                pool.memset(idente[:, :], 0.0).then_inc(e_z, 1)
                pool.memset(before[:, :], 1.0).then_inc(e_z, 1)
                pool.wait_ge(e_z, 2)
                pool.affine_select(out=idente[:, :], in_=idente[:, :], compare_op=ALU.not_equal, fill=1.0,
                                   base=0, pattern=[[-1, P]], channel_multiplier=1).then_inc(e_id, 1)
                pool.affine_select(out=before[:, :], in_=before[:, :], compare_op=ALU.is_gt, fill=0.0,
                                   base=S, pattern=[[-1, 2 * S]], channel_multiplier=1).then_inc(e_id, 1)

            @block.scalar
            def _(a):
                s = nc.scalar
                s.preload_act_table_set("natural_log_exp_and_others")
                for j in range(TILES):
                    a.wait_ge(e_mv, j + 1)
                    s.activation(rs_e[:, j:j + 1], mv_e[:, j, 1:2], ACT.Ln, bias=eps_e[:, 0:1]).then_inc(e_ln, 1)
                    a.wait_ge(e_ln, j + 1)
                    s.activation(rs_e[:, j:j + 1], rs_e[:, j:j + 1], ACT.Exp, scale=-0.5).then_inc(e_rs, 1)
                a.wait_ge(e_max, 2)
                s.activation(le[:, :, :], le[:, :, :], ACT.Exp).then_inc(e_exp, 1)
                a.wait_ge(e_btc, 1)
                for e in range(E):
                    if e >= 2:
                        a.wait_ge(e_y, (e - 1) * TILES)
                    for c in range(FC):
                        for h in range(S // HALF):
                            n = (e * FC + c) * 2 + h
                            a.wait_ge(e_h, n + 1)
                            s.activation(hid[:, e % 2, c, h * HALF:(h + 1) * HALF], HP[n % 4][:, :], ACT.Relu,
                                         bias=b1t[:, e * FC + c:e * FC + c + 1]).then_inc(e_hr, 1)
                for j in range(TILES):
                    a.wait_ge(e_mv2, j + 1)
                    s.activation(rs_e[:, j:j + 1], mv_e[:, j, 1:2], ACT.Ln, bias=eps_e[:, 0:1]).then_inc(e_ln2, 1)
                    a.wait_ge(e_ln2, j + 1)
                    s.activation(rs_e[:, j:j + 1], rs_e[:, j:j + 1], ACT.Exp, scale=-0.5).then_inc(e_rs2, 1)

            @block.tensor
            def _(pe):
                pe.wait_ge(e_id, 1)
                pe.wait_ge(e_w, 16 * NW)
                pe.transpose(TE[0][:, 0:E], rwn[:, :], idente[0:E, 0:E])
                pe.transpose(TE[0][:, E:E + E * FC], b1n[:, :], idente[0:E * FC, 0:E * FC]).then_inc(e_bt, 1)
                for j in range(TILES):
                    pe.wait_ge(e_xb, j + 1)
                    if j >= 2:
                        pe.wait_ge(e_tc, j - 1)
                    else:
                        pe.wait_ge(e_btc, 1)
                    pe.transpose(TE[j % 2][:, 0:P], xb[:, j, :], idente[:, :]).then_inc(e_t, 1)
                pe.wait_ge(e_tc, TILES)
                for j in range(TILES):
                    mm = pe.matmul(YE[0][:, j * E:(j + 1) * E], xbt[:, j * P:(j + 1) * P], rwt[:, :], start=True, stop=True)
                mm.then_inc(e_lg, 1)

                def hidden(e):
                    pe.wait_ge(e_w2, 32 * E)
                    for c in range(FC):
                        for h in range(S // HALF):
                            n = (e * FC + c) * 2 + h
                            if n >= 4:
                                pe.wait_ge(e_hr, n - 3)
                            pe.matmul(HP[n % 4][:, :], w1[:, e, c * P:(c + 1) * P], xbt[:, h * HALF:(h + 1) * HALF],
                                      start=True, stop=True).then_inc(e_h, 1)

                hidden(0)
                pe.wait_ge(e_lgc, 1)
                for e in range(E):
                    if e + 1 < E:
                        hidden(e + 1)
                    pe.wait_ge(e_hr, (e + 1) * FC * 2)
                    for j in range(TILES):
                        n = e * TILES + j
                        if n >= 2:
                            pe.wait_ge(e_ya, n - 1)
                        pe.matmul(YE[n % 2][:, 0:D], ones[:, :], b2r[:, e, :], start=True, stop=False)
                        for c in range(FC):
                            mm = pe.matmul(YE[n % 2][:, 0:D], hid[:, e % 2, c, j * P:(j + 1) * P], w2[:, e, c, :],
                                           start=False, stop=(c == FC - 1))
                        mm.then_inc(e_y, 1)

            @block.vector
            def _(dve):
                v = nc.vector
                v.memset(eps_e[:, :], EPS)
                v.memset(ones[:, :], 1.0).then_inc(e_wg, 1)
                for e in range(E):
                    v.memset(weigh[:, e:e + 1], float(E - e)).then_inc(e_wg, 1)
                dve.wait_ge(e_bt, 1)
                v.tensor_copy(rwt[:, :], TE[0][:, 0:E])
                v.tensor_copy(b1t[:, :], TE[0][:, E:E + E * FC]).then_inc(e_btc, 1)
                dve.wait_ge(e_x, 32)
                dve.wait_ge(e_w, 16 * NW)
                for j in range(TILES):
                    v.tensor_tensor(ya[:, j, :], ya[:, j, :], bo_r[:, :], ALU.add).then_inc(e_add, 1)
                    dve.wait_ge(e_add, j + 1)
                    v.tensor_tensor(xb[:, j, :], xb[:, j, :], ya[:, j, :], ALU.add).then_inc(e_add2, 1)
                    dve.wait_ge(e_add2, j + 1)
                    v.bn_stats(st_e[:, j, :], xb[:, j, :]).then_inc(e_st, 1)
                    dve.wait_ge(e_st, j + 1)
                    v.bn_aggr(mv_e[:, j, :], st_e[:, j, :]).then_inc(e_mv, 1)
                for j in range(TILES):
                    dve.wait_ge(e_mv, j + 1)
                    dve.wait_ge(e_rs, j + 1)
                    v.tensor_scalar(xb[:, j, :], xb[:, j, :], mv_e[:, j, 0:1], rs_e[:, j:j + 1],
                                    ALU.subtract, ALU.mult).then_inc(e_xb, 1)
                for j in range(TILES):
                    dve.wait_ge(e_t, j + 1)
                    v.tensor_copy(xbt[:, j * P:(j + 1) * P], TE[j % 2][:, 0:P]).then_inc(e_tc, 1)
                dve.wait_ge(e_lg, 1)
                v.tensor_copy(lg[:, :, :].rearrange("p j e -> p (j e)"), YE[0][:, 0:TILES * E]).then_inc(e_lgc, 1)
                dve.wait_ge(e_lgc, 1)
                v.tensor_reduce(lmax[:, :], lg[:, :, :], AX_X, ALU.max).then_inc(e_max, 1)
                dve.wait_ge(e_max, 1)
                mb = lmax[:, :].unsqueeze(2).broadcast_to([P, TILES, E])
                v.tensor_tensor(le[:, :, :], lg[:, :, :], mb, ALU.subtract).then_inc(e_max, 1)
                v.tensor_tensor(cand[:, :, :], lg[:, :, :], mb, ALU.is_ge).then_inc(e_c, 1)
                dve.wait_ge(e_c, 1)
                v.tensor_tensor(cand[:, :, :], cand[:, :, :], weigh[:, :].unsqueeze(1).broadcast_to([P, TILES, E]),
                                ALU.mult).then_inc(e_c2, 1)
                dve.wait_ge(e_c2, 1)
                v.tensor_reduce(idx[:, :], cand[:, :, :], AX_X, ALU.max).then_inc(e_i0, 1)
                dve.wait_ge(e_i0, 1)
                v.tensor_scalar(idx[:, :], idx[:, :], -1.0, float(E), ALU.mult, ALU.add).then_inc(e_i, 1)
                dve.wait_ge(e_exp, 1)
                v.tensor_reduce(lsum[:, :], le[:, :, :], AX_X, ALU.add).then_inc(e_sum, 1)
                dve.wait_ge(e_sum, 1)
                v.reciprocal(prob[:, :], lsum[:, :]).then_inc(e_p, 1)
                dve.wait_ge(e_row, 32)
                dve.wait_ge(e_p, 1)
                dve.wait_ge(e_id, 2)
                for j in range(TILES):
                    if j:
                        dve.wait_ge(e_rk, j)
                    v.tensor_scalar(beat[:, :], prow[:, :], prob[:, j:j + 1], None, ALU.is_gt).then_inc(e_g, 1)
                    v.scalar_tensor_tensor(out=tie[:, :], in0=prow[:, :], scalar=prob[:, j:j + 1],
                                           in1=before[:, S - j * P:2 * S - j * P], op0=ALU.is_equal,
                                           op1=ALU.mult).then_inc(e_tie, 1)
                    dve.wait_ge(e_tie, j + 1)
                    v.tensor_tensor(beat[:, :], beat[:, :], tie[:, :], ALU.add).then_inc(e_b, 1)
                    dve.wait_ge(e_b, j + 1)
                    v.scalar_tensor_tensor(out=tie[:, :], in0=irow[:, :], scalar=idx[:, j:j + 1], in1=beat[:, :],
                                           op0=ALU.is_equal, op1=ALU.mult, accum_out=rank[:, j:j + 1]).then_inc(e_rk, 1)
                dve.wait_ge(e_rk, TILES)
                v.tensor_scalar(kept[:, :], rank[:, :], float(CAP), None, ALU.is_lt).then_inc(e_kp, 1)
                dve.wait_ge(e_kp, 1)
                v.tensor_tensor(fin_e[:, :], idx[:, :], kept[:, :], ALU.mult).then_inc(e_fe, 1)
                dve.wait_ge(e_fe, 1)
                for e in range(E):
                    ins = v.tensor_scalar(mask[:, :, e], fin_e[:, :], float(e), None, ALU.is_equal)
                ins.then_inc(e_mk, 1)
                dve.wait_ge(e_mk, 1)
                for e in range(E):
                    for j in range(TILES):
                        n = e * TILES + j
                        dve.wait_ge(e_y, n + 1)
                        if e:
                            dve.wait_ge(e_ya, n - TILES + 1)
                        v.scalar_tensor_tensor(out=acc[:, j, :], in0=YE[n % 2][:, 0:D], scalar=mask[:, j, e:e + 1],
                                               in1=acc[:, j, :] if e else xb[:, j, :],
                                               op0=ALU.mult, op1=ALU.add).then_inc(e_ya, 1)
                for j in range(TILES):
                    dve.wait_ge(e_ya, (E - 1) * TILES + j + 1)
                    v.bn_stats(st_e[:, j, :], acc[:, j, :]).then_inc(e_st2, 1)
                    dve.wait_ge(e_st2, j + 1)
                    v.bn_aggr(mv_e[:, j, :], st_e[:, j, :]).then_inc(e_mv2, 1)
                for j in range(TILES):
                    dve.wait_ge(e_mv2, j + 1)
                    dve.wait_ge(e_rs2, j + 1)
                    v.tensor_scalar(acc[:, j, :], acc[:, j, :], mv_e[:, j, 0:1], rs_e[:, j:j + 1],
                                    ALU.subtract, ALU.mult).then_inc(e_fin, 1)


_INS = ["x", "ctx_768", "L0_attn_ln1_w", "L0_attn_conv_w", "L0_attn_conv_b", "L0_attn_wi", "L0_attn_wf", "L0_attn_wz",
        "L0_attn_wo", "L0_attn_rker", "L0_attn_cell_b", "L0_attn_gn_w", "L0_attn_ln2_w", "L0_attn_ff_up",
        "L0_attn_ff_down", "L0_attn_post_w", "L0_xattn_Wq", "L0_xattn_Wk", "L0_xattn_Wv", "L0_xattn_Wo",
        "L0_xattn_bo", "L0_ffn_router_w", "L0_ffn_W1", "L0_ffn_b1", "L0_ffn_W2", "L0_ffn_b2"]


def decoder_kernel(nc, t, out):
    _, S, D = t["x"].shape
    NK, DC = t["ctx_768"].shape[1:]
    L, H, DH, _ = t["L0_attn_wi"].shape
    K = t["L0_attn_conv_w"].shape[2]
    UP = t["L0_attn_ff_down"].shape[1]
    E, _, FF = t["L0_ffn_W1"].shape
    DHEAD = 64
    HEADS = t["L0_xattn_Wq"].shape[1] // DHEAD
    rows = S + (2 * (L - 1) + 1) * Q
    x = t["x"].rearrange("b s d -> (b s) d")
    scr_in = nc.dram_tensor("scr_in", [rows + Q, D], F32).ap()
    scr_out = nc.dram_tensor("scr_out", [rows, D], F32).ap()
    xa = nc.dram_tensor("scr_xa", [S, D], F32).ap()
    att = nc.dram_tensor("scr_att", [S, D], F32).ap()
    row_p = nc.dram_tensor("scr_p", [S], F32).ap()
    row_i = nc.dram_tensor("scr_i", [S], F32).ap()
    slstm_stage(nc, x, {n[8:]: t[n] for n in _INS if n.startswith("L0_attn_")}, scr_in, scr_out,
                (S, D, L, H, K, UP))
    xw = {n[9:]: t[n] for n in _INS if n.startswith("L0_xattn_")}
    xw["post_w"] = t["L0_attn_post_w"]
    attention_stage(nc, x, t["ctx_768"].rearrange("b s d -> (b s) d"), xw, scr_out, rows - S, att, xa,
                    (S, D, HEADS, DHEAD, NK, DC))
    capacity = -(-S * 5 // (4 * E))
    experts_stage(nc, att, xa, {n[7:]: t[n] for n in _INS if n.startswith("L0_ffn_")}, t["L0_xattn_bo"],
                  row_p, row_i, out.rearrange("b s d -> (b s) d"), (S, D, E, FF, capacity))


def kernel(**inputs):
    from concourse import bacc
    from concourse.bass_utils import run_bass_kernel_spmd

    nc = bacc.Bacc("TRN2", target_bir_lowering=False, num_devices=1)
    arrays, t = {}, {}
    for name in _INS:
        a = np.ascontiguousarray(inputs[name])
        arrays["in_" + name] = a
        t[name] = nc.dram_tensor("in_" + name, a.shape, mybir.dt.from_np(a.dtype), kind="ExternalInput").ap()
    out = nc.dram_tensor("out_dram", t["x"].shape, F32, kind="ExternalOutput").ap()
    decoder_kernel(nc, t, out)
    r = run_bass_kernel_spmd(nc, [arrays], core_ids=[0])
    return r.results[0]["out_dram"]
```

```python
from contextlib import ExitStack

import numpy as np
import concourse.bass as bass
from concourse import mybir

ALU = mybir.AluOpType
ACT = mybir.ActivationFunctionType
AX_X = mybir.AxisListType.X
F32 = mybir.dt.float32
F16 = mybir.dt.float16
BF16 = mybir.dt.bfloat16

P = 128
Q = 32
EPS = 1e-5
H_SCALE = 2.0 ** 12
R_SCALE = 2.0 ** 8
G_SCALE = H_SCALE * R_SCALE
M_SCALE = 2.0 ** 6
M_START = -32.0
LN_LOW = 2.0 ** -63
E_TOP = 2.0 ** 40


def slstm_stage(nc, x, w, scratch_in, scratch_out, dims):
    S, D, L, H, K, UP = dims
    DH = D // H
    CH = P // L
    C = L * H
    LAG = 2
    NCH = S // CH
    ITERS = NCH + LAG * (L - 1)
    assert ITERS % 2 == 0
    assert DH == Q and CH == Q and D == P and CH * C == 512

    with ExitStack() as ctx:
        def sb(name, shape, dt=F32):
            return ctx.enter_context(nc.sbuf_tensor(name, shape, dt))

        def ps(name, shape, dt=F32):
            return ctx.enter_context(nc.psum_tensor(name, shape, dt))

        sems = []

        def sem(name):
            s = ctx.enter_context(nc.semaphore(name))
            sems.append(s)
            return s

        ident = sb("ident", [P, P])
        gate_w = sb("gate_w", [P, L, H, 4, Q])
        gate_b = sb("gate_b", [P, 4, Q])
        pick = sb("pick", [P, CH, C])
        rec_w = sb("rec_w", [P, C, P], F16)
        m_eye = sb("m_eye", [P, P], F16)
        up_w = sb("up_w", [P, L, 2 * UP])
        dn_w0 = sb("dn_w0", [P, L, D])
        dn_w1 = sb("dn_w1", [UP - P, L, D])
        conv_w = sb("conv_w", [P, L, K])
        conv_b = sb("conv_b", [P, L])
        ln1_w = sb("ln1_w", [P, L])
        ln2_w = sb("ln2_w", [P, L])
        gn_w = sb("gn_w", [P, D])
        eps_ln = sb("eps_ln", [P, 1])
        eps_gn = sb("eps_gn", [P, 1])
        keep = sb("keep", [P, ITERS + 1, C])
        xin = [sb(f"xin{i}", [P, D]) for i in range(2)]
        x1 = sb("x1", [P, D])
        x2 = sb("x2", [P, D])
        stats = sb("stats", [P, 6])
        mv = sb("mv", [P, 2])
        lnv = sb("lnv", [P, H])
        rstd = sb("rstd", [P, H])
        normed = sb("normed", [P, D])
        xn = sb("xn", [P, L, K - 1 + CH])
        taps = sb("taps", [P, K, L, CH])
        cv = sb("cv", [P, L, CH])
        cv2 = sb("cv2", [P, L, CH])
        sg = sb("sg", [P, L, CH])
        sg1 = sb("sg1", [P, L, CH])
        sr = sb("sr", [P, L, CH])
        xc = sb("xc", [P, L, CH])
        yt = sb("yt", [P, H, Q])
        yc = sb("yc", [P, H, Q])
        ysq = sb("ysq", [P, H, Q])
        ysum = sb("ysum", [P, H])
        yvar = sb("yvar", [P, H])
        yg = sb("yg", [P, D])
        n2t = sb("n2t", [P, L, CH])
        gl = sb("gl", [P, UP])
        act = sb("act", [P, UP])
        at0 = sb("at0", [P, P])
        at1 = sb("at1", [UP - P, P])
        eb = sb("eb", [Q, C])
        ex = sb("ex", [Q, 3 * C])
        ad = sb("ad", [Q, 3 * C])
        tt = sb("tt", [Q, 3 * C])
        p1 = sb("p1", [Q, C])
        p2 = sb("p2", [Q, C])
        rp = sb("rp", [Q, C])
        a1 = sb("a1", [Q, C])
        a2 = sb("a2", [Q, C])
        nn = sb("nn", [Q, C])
        ll = sb("ll", [Q, 2 * C])
        i64 = sb("i64", [Q, C])
        vv = sb("vv", [Q, C])
        m64 = sb("m64", [Q, C])
        hb = [sb(f"hb{i}", [Q, CH + 1, 2 * C]) for i in range(2)]
        st = sb("st", [P, C], F16)
        ms = sb("ms", [P, C], F16)
        kb = sb("kb", [Q, C])

        G = [ps(f"G{i}", [P, CH, C]) for i in range(2)]
        TP = ps("TP", [P, 512])
        U = ps("U", [P, 512])
        FD = ps("FD", [P, 512])
        TG = ps("TG", [P, 4, P])

        with ExitStack() as c2:
            def sb2(name, shape, dt=F32):
                return c2.enter_context(nc.sbuf_tensor(name, shape, dt))
            nat = sb2("nat", [P, L, 4, P])
            rnat = sb2("rnat", [3 * Q, C, 4, Q])
            rcmb = sb2("rcmb", [3 * Q, C, 4, Q])
            bnat = sb2("bnat", [C, 4, Q])
            d_nat = sem("d_nat")
            d_rec = sem("d_rec")
            d_w = sem("d_w")
            z_nat = sem("z_nat")
            z_id = sem("z_id")
            z_sel = sem("z_sel")
            z_pe = sem("z_pe")
            z_ev = sem("z_ev")
            z_rc = sem("z_rc")
            z_hi = sem("z_hi")
            z_init = sem("z_init")
            z_me = sem("z_me")
            with nc.Block() as block:
                N_W = 0

                @block.sync
                def _(sp):
                    nonlocal N_W
                    sp.wait_ge(z_nat, 1)
                    n = 0
                    for g, name in enumerate(("wi", "wf", "wz", "wo")):
                        for h in range(H):
                            sp.dma_start(nat[h * Q:(h + 1) * Q, :, g, h * Q:(h + 1) * Q],
                                         w[name][:, h, :, :].rearrange("l o d -> o l d")).then_inc(d_nat, 16)
                    for c in range(3):
                        sp.dma_start(rnat[c * Q:(c + 1) * Q, :, :, :],
                                     w["rker"].rearrange("l h d g o -> d (l h) g o")).then_inc(d_rec, 16)
                    loads = [
                        (up_w[:, :, :], w["ff_up"].rearrange("l d u -> d l u")),
                        (dn_w0[:, :, :], w["ff_down"][:, 0:P, :].rearrange("l u d -> u l d")),
                        (dn_w1[:, :, :], w["ff_down"][:, P:UP, :].rearrange("l u d -> u l d")),
                        (conv_w[:, :, :], w["conv_w"].rearrange("l d k -> d l k")),
                        (conv_b[:, :], w["conv_b"].rearrange("l d -> d l")),
                        (ln1_w[:, :], w["ln1_w"].rearrange("l d -> d l")),
                        (ln2_w[:, :], w["ln2_w"].rearrange("l d -> d l")),
                        (bnat[:, :, :], w["cell_b"].rearrange("l h g o -> (l h) g o")),
                        (scratch_in[0:S, :], x),
                        (scratch_in[S:(ITERS + 2) * CH, :], x[0:(ITERS + 2) * CH - S, :]),
                        (xin[0][0:Q, :], x[0:CH, :]),
                        (xin[1][0:Q, :], x[CH:2 * CH, :]),
                    ]
                    loads += [(gn_w[l * CH:(l + 1) * CH, :], w["gn_w"][l:l + 1, :].broadcast_to([CH, D])) for l in range(L)]
                    for dst, src in loads:
                        sp.dma_start(dst, src, allow_slow_non_contiguous=True).then_inc(d_w, 16)
                    sp.wait_ge(d_w, 16 * len(loads))

                @block.gpsimd
                def _(pool):
                    pool.memset(nat[:, :, :, :], 0.0).then_inc(z_nat, 1)
                    pool.memset(ident[:, :], 0.0).then_inc(z_id, 1)
                    pool.memset(pick[:, :, :], 0.0).then_inc(z_id, 1)
                    pool.wait_ge(z_id, 2)
                    pool.affine_select(out=ident[:, :], in_=ident[:, :], compare_op=ALU.not_equal, fill=1.0,
                                       base=0, pattern=[[-1, P]], channel_multiplier=1).then_inc(z_sel, 1)
                    pool.affine_select(out=pick[:, :, :], in_=pick[:, :, :], compare_op=ALU.not_equal, fill=1.0,
                                       base=0, pattern=[[0, CH], [-1, C]], channel_multiplier=1).then_inc(z_sel, 1)

                @block.tensor
                def _(pe):
                    pe.wait_ge(d_nat, 16 * 4 * H)
                    pe.wait_ge(z_sel, 1)
                    for l in range(L):
                        if l:
                            pe.wait_ge(z_ev, l)
                        for g in range(4):
                            last = pe.transpose(TG[:, g, :], nat[:, l, g, :], ident[:, :])
                        last.then_inc(z_pe, 1)

                @block.vector
                def _(dve):
                    v = nc.vector
                    v.memset(gate_b[:, :, :], 0.0).then_inc(z_init, 1)
                    v.memset(keep[:, :, :], 1.0).then_inc(z_init, 1)
                    v.memset(eps_ln[:, :], EPS)
                    v.memset(eps_gn[:, :], EPS * H_SCALE * H_SCALE)
                    v.memset(xn[:, :, :], 0.0)
                    v.memset(ad[:, :], 1.0)
                    v.memset(hb[0][:, :, :], 0.0)
                    v.memset(hb[1][:, :, :], 0.0)
                    v.memset(st[:, :], 0.0)
                    v.memset(ms[:, :], 0.0)
                    v.memset(m64[:, :], 0.0)
                    for q in range(1, L):
                        v.memset(xin[0][q * Q:(q + 1) * Q, :], 0.0)
                        v.memset(xin[1][q * Q:(q + 1) * Q, :], 0.0)
                    v.memset(m_eye[:, :], 0.0).then_inc(z_init, 1)
                    v.memset(rec_w[:, :, :], 0.0).then_inc(z_init, 1)
                    dve.wait_ge(z_init, 4)
                    for l in range(L):
                        v.memset(keep[:, LAG * l, l * H:(l + 1) * H], 0.0)
                    dve.wait_ge(z_sel, 1)
                    for q in range(2):
                        for g in range(2):
                            v.tensor_scalar(m_eye[q * Q:(q + 1) * Q, g * Q:(g + 1) * Q],
                                            ident[q * Q:(q + 1) * Q, q * Q:(q + 1) * Q],
                                            -G_SCALE / M_SCALE, None, ALU.mult)
                    for l in range(L):
                        dve.wait_ge(z_pe, l + 1)

                        def tg(g):
                            return TG[:, g, :].rearrange("p (h o) -> p h o", h=H)
                        v.tensor_scalar(gate_w[:, l, :, 0, :], tg(0), G_SCALE, None, ALU.mult).then_inc(z_me, 1)
                        v.tensor_scalar(gate_w[:, l, :, 2, :], tg(2), 2.0 * G_SCALE, None, ALU.mult)
                        v.tensor_scalar(gate_w[:, l, :, 3, :], tg(3), -G_SCALE, None, ALU.mult)
                        dve.wait_ge(z_me, l + 1)
                        v.scalar_tensor_tensor(out=gate_w[:, l, :, 1, :], in0=tg(1), scalar=-G_SCALE,
                                               in1=gate_w[:, l, :, 0, :], op0=ALU.mult, op1=ALU.add).then_inc(z_ev, 1)
                    dve.wait_ge(d_rec, 48)
                    cr = R_SCALE
                    v.tensor_scalar(rcmb[:, :, 0, :], rnat[:, :, 0, :], cr, None, ALU.mult).then_inc(z_rc, 1)
                    v.tensor_scalar(rcmb[:, :, 2, :], rnat[:, :, 2, :], 2.0 * cr, None, ALU.mult)
                    v.tensor_scalar(rcmb[:, :, 3, :], rnat[:, :, 3, :], -cr, None, ALU.mult)
                    dve.wait_ge(z_rc, 1)
                    v.scalar_tensor_tensor(out=rcmb[:, :, 1, :], in0=rnat[:, :, 1, :], scalar=-cr,
                                           in1=rcmb[:, :, 0, :], op0=ALU.mult, op1=ALU.add).then_inc(z_rc, 1)
                    dve.wait_ge(z_rc, 2)
                    v.tensor_copy(rec_w[0:3 * Q, :, :], rcmb[:, :, :, :].rearrange("p c g o -> p c (g o)")).then_inc(z_hi, 1)
                    dve.wait_ge(z_hi, 1)
                    v.tensor_tensor(rec_w[2 * Q:3 * Q, :, :],
                                    rcmb[2 * Q:3 * Q, :, :, :].rearrange("p c g o -> p c (g o)"),
                                    rec_w[2 * Q:3 * Q, :, :], ALU.subtract)
                    dve.wait_ge(d_w, 16 * (12 + L))
                    v.tensor_scalar(gate_b[0:C, 0, :], bnat[:, 0, :], G_SCALE, None, ALU.mult).then_inc(z_rc, 1)
                    v.tensor_scalar(gate_b[0:C, 2, :], bnat[:, 2, :], 2.0 * G_SCALE, None, ALU.mult)
                    v.tensor_scalar(gate_b[0:C, 3, :], bnat[:, 3, :], -G_SCALE, None, ALU.mult)
                    dve.wait_ge(z_rc, 3)
                    v.scalar_tensor_tensor(out=gate_b[0:C, 1, :], in0=bnat[:, 1, :], scalar=-G_SCALE,
                                           in1=gate_b[0:C, 0, :], op0=ALU.mult, op1=ALU.add)

        pre_ready, b_ready, gates_ready, bc_ready, t_ready = (
            sem(n) for n in ("pre_ready", "b_ready", "gates_ready", "bc_ready", "t_ready"))
        p1_ready, a_ready, p2_ready, r_ready = (sem(n) for n in ("p1_ready", "a_ready", "p2_ready", "r_ready"))
        h_ready, y_ready, h_split = (sem(n) for n in ("h_ready", "y_ready", "h_split"))
        ln_ready, m_ready, m_split = (sem(n) for n in ("ln_ready", "m_ready", "m_split"))
        B = {n: sem(n) for n in (
            "st1 mv1 ln1 rs1 nm1 tp1 hist xn1 tap add1 add2 cvb sge sg1 srr xcr "
            "yt ysum ymean yc ysq yvar gln grs gnm gnw x1r st2 mv2 ln2 rs2 nm2 tp2 n2r upr glr acr tpa atr dnr x2r ini mks"
        ).split()}
        d_xin, d_out = sem("d_xin"), sem("d_out")

        def bc(ap, n):
            return ap.unsqueeze(2).broadcast_to([*ap.shape, n])

        def by_layer(ap):
            return ap.rearrange("p (l t) -> p l t", l=L)

        def keep_at(parts, c):
            return keep[parts, bass.ds(c, 1), :].rearrange("p a c -> p (a c)")

        def norm_scale(a, var, n, scale, eps, var_ready, ln_done, rs_done, k):
            a.wait_ge(var_ready, k)
            nc.scalar.activation(lnv[:, 0:n], var, ACT.Ln, bias=eps[:, 0:1], scale=scale).then_inc(ln_done, 1)
            a.wait_ge(ln_done, k)
            nc.scalar.activation(rstd[:, 0:n], lnv[:, 0:n], ACT.Exp, scale=-0.5).then_inc(rs_done, 1)

        def dve_stats(dve, src, st_done, mv_done, k):
            nc.vector.bn_stats(stats[:, :], src).then_inc(st_done, 1)
            dve.wait_ge(st_done, k)
            nc.vector.bn_aggr(mv[:, :], stats[:, :]).then_inc(mv_done, 1)

        def dve_norm(dve, src, mv_done, rs_done, nm_done, k):
            dve.wait_ge(mv_done, k)
            dve.wait_ge(rs_done, k)
            nc.vector.tensor_scalar(normed[:, :], src, mv[:, 0:1], rstd[:, 0:1],
                                    ALU.subtract, ALU.mult).then_inc(nm_done, 1)

        def dve_xn(dve, k):
            dve.wait_ge(B["tp1"], k)
            dve.wait_ge(B["hist"], k)
            nc.vector.tensor_tensor(xn[:, :, K - 1:K - 1 + CH], by_layer(TP[:, 0:P]),
                                    bc(ln1_w[:, :], CH), ALU.mult).then_inc(B["xn1"], 1)

        def pool_history(pool, c):
            nc.gpsimd.tensor_tensor(xn[:, :, 0:K - 1], xn[:, :, CH:CH + K - 1],
                                    bc(keep[:, bass.ds(c, 1), 0:C:H].rearrange("p a l -> p (a l)"), K - 1),
                                    ALU.mult).then_inc(B["hist"], 1)

        def pool_conv(pool, k):
            pool.wait_ge(B["xn1"], k)
            for j in range(K):
                nc.gpsimd.tensor_tensor(taps[:, j, :, :], xn[:, :, j:j + CH], bc(conv_w[:, :, j], CH),
                                        ALU.mult).then_inc(B["tap"], 1)
            pool.wait_ge(B["tap"], K * (k - 1) + 2)
            nc.gpsimd.tensor_tensor(cv[:, :, :], taps[:, 0, :, :], taps[:, 1, :, :], ALU.add).then_inc(B["add1"], 1)
            pool.wait_ge(B["tap"], K * k)
            nc.gpsimd.tensor_tensor(cv2[:, :, :], taps[:, 2, :, :], taps[:, 3, :, :], ALU.add).then_inc(B["add1"], 1)
            pool.wait_ge(B["add1"], 2 * k)
            nc.gpsimd.tensor_tensor(cv[:, :, :], cv[:, :, :], cv2[:, :, :], ALU.add).then_inc(B["add2"], 1)
            pool.wait_ge(B["add2"], k)
            nc.gpsimd.tensor_tensor(cv2[:, :, :], cv[:, :, :], bc(conv_b[:, :], CH), ALU.add).then_inc(B["cvb"], 1)
            pool.wait_ge(B["sge"], k)
            nc.gpsimd.tensor_scalar(sg1[:, :, :], sg[:, :, :], 1.0, None, ALU.add).then_inc(B["sg1"], 1)

        def act_silu(a, k):
            a.wait_ge(B["cvb"], k)
            nc.scalar.activation(sg[:, :, :], cv2[:, :, :], ACT.Exp, scale=-1.0).then_inc(B["sge"], 1)

        def dve_silu(dve, k, half):
            dve.wait_ge(B["sg1"], k)
            a, b = half * L // 2, (half + 1) * L // 2
            nc.vector.reciprocal(sr[:, a:b, :], sg1[:, a:b, :]).then_inc(B["srr"], 1)

        def pool_silu(pool, k):
            pool.wait_ge(B["srr"], 2 * k)
            nc.gpsimd.tensor_tensor(xc[:, :, :], cv2[:, :, :], sr[:, :, :], ALU.mult).then_inc(B["xcr"], 1)

        def pe_norm_t(pe, nm_done, tp_done, k):
            pe.wait_ge(nm_done, k)
            pe.transpose(TP[:, 0:P], normed[:, :], ident[:, :]).then_inc(tp_done, 1)

        def pe_gate_bias(pe, g):
            pe.matmul(g[:, :, :].rearrange("p t c -> p (t c)"), gate_b[:, :, :].rearrange("p g o -> p (g o)"),
                      pick[:, :, :].rearrange("p t c -> p (t c)"), start=True, stop=False, skip_group_check=True)

        def pe_gates(pe, g, k, l, conv):
            pe.wait_ge(B["xcr"] if conv else B["xn1"], k)
            g0 = 0 if conv else 2
            for h in range(H):
                rhs = xc[:, l, :] if conv else xn[:, l, K - 1:K - 1 + CH]
                mm = pe.matmul(g[g0 * Q:(g0 + 2) * Q, :, l * H + h],
                               gate_w[:, l, h, g0:g0 + 2, :].rearrange("p g o -> p (g o)"),
                               rhs, start=False, stop=False, skip_group_check=True)
            return mm

        def dve_heads(dve, old):
            for l in range(L):
                ins = nc.vector.transpose(yt[l * CH:(l + 1) * CH, :, :],
                                          old[:, 1:CH + 1, l * H:(l + 1) * H].rearrange("p t h -> p h t"))
            ins.then_inc(B["yt"], 1)

        def dve_head_sum(dve, k):
            dve.wait_ge(B["yt"], k)
            nc.vector.tensor_reduce(ysum[:, :], yt[:, :, :], AX_X, ALU.add).then_inc(B["ysum"], 1)

        def dve_head_var(dve, k):
            dve.wait_ge(B["ysq"], k)
            nc.vector.tensor_reduce(yvar[:, :], ysq[:, :, :], AX_X, ALU.add).then_inc(B["yvar"], 1)

        def pool_heads(pool, residual, k):
            pl = nc.gpsimd
            pool.wait_ge(B["ysum"], k)
            pl.tensor_scalar(ysum[:, :], ysum[:, :], -1.0 / DH, None, ALU.mult).then_inc(B["ymean"], 1)
            pool.wait_ge(B["ymean"], k)
            pl.tensor_tensor(yc[:, :, :], yt[:, :, :], bc(ysum[:, :], DH), ALU.add).then_inc(B["yc"], 1)
            pool.wait_ge(B["yc"], k)
            pl.tensor_tensor(ysq[:, :, :], yc[:, :, :], yc[:, :, :], ALU.mult).then_inc(B["ysq"], 1)
            pool.wait_ge(B["grs"], k)
            pl.tensor_tensor(yt[:, :, :], yc[:, :, :], bc(rstd[:, :], DH), ALU.mult).then_inc(B["gnm"], 1)
            pool.wait_ge(B["gnm"], k)
            pl.tensor_tensor(yg[:, :], yt[:, :, :].rearrange("p h o -> p (h o)"), gn_w[:, :],
                             ALU.mult).then_inc(B["gnw"], 1)
            pool.wait_ge(B["gnw"], k)
            pl.tensor_tensor(x1[:, :], residual, yg[:, :], ALU.add).then_inc(B["x1r"], 1)

        def act_gelu(a, k):
            a.wait_ge(B["upr"], k)
            nc.scalar.activation(gl[:, :], U[:, 0:UP], ACT.Gelu).then_inc(B["glr"], 1)
            nc.scalar.preload_act_table_set("natural_log_exp_and_others")

        def dve_n2(dve, k):
            dve.wait_ge(B["tp2"], k)
            nc.vector.tensor_tensor(n2t[:, :, :], by_layer(TP[:, 0:P]), bc(ln2_w[:, :], CH),
                                    ALU.mult).then_inc(B["n2r"], 1)

        def dve_gated(dve, k):
            dve.wait_ge(B["glr"], k)
            nc.vector.tensor_tensor(act[:, :], U[:, UP:2 * UP], gl[:, :], ALU.mult).then_inc(B["acr"], 1)

        def dve_gated_t(dve, k):
            dve.wait_ge(B["tpa"], k)
            nc.vector.tensor_copy(at0[:, :], TP[:, 0:P])
            nc.vector.tensor_copy(at1[:, :], TP[0:UP - P, P:2 * P]).then_inc(B["atr"], 1)

        def dve_out(dve, k):
            dve.wait_ge(B["dnr"], k)
            nc.vector.tensor_tensor(x2[:, :], FD[:, 0:D], x1[:, :], ALU.add).then_inc(B["x2r"], 1)

        def pe_up(pe, k, layers):
            pe.wait_ge(B["n2r"], k)
            for l in layers:
                mm = pe.matmul(U[l * CH:(l + 1) * CH, 0:2 * UP], n2t[:, l, :], up_w[:, l, :], start=True, stop=True)
            return mm

        def pe_gated_t(pe, k):
            pe.wait_ge(B["acr"], k)
            pe.transpose(TP[:, 0:P], act[:, 0:P], ident[:, :])
            pe.transpose(TP[0:UP - P, P:2 * P], act[:, P:UP], ident[:, :]).then_inc(B["tpa"], 1)

        def pe_down(pe, k, layers):
            pe.wait_ge(B["atr"], k)
            for l in layers:
                pe.matmul(FD[l * CH:(l + 1) * CH, 0:D], at0[:, l * CH:(l + 1) * CH], dn_w0[:, l, :],
                          start=True, stop=False)
                mm = pe.matmul(FD[l * CH:(l + 1) * CH, 0:D], at1[:, l * CH:(l + 1) * CH], dn_w1[:, l, :],
                               start=False, stop=True)
            return mm

        with nc.Block() as block:
            @block.gpsimd
            def _(pool):
                pool_history(pool, 0)
                pool_conv(pool, 1)
                pool_silu(pool, 1)

            @block.scalar
            def _(a):
                nc.scalar.preload_act_table_set("natural_log_exp_and_others")
                norm_scale(a, mv[:, 1:2], 1, 1.0, eps_ln, B["mv1"], B["ln1"], B["rs1"], 1)
                act_silu(a, 1)

            @block.vector
            def _(dve):
                dve_stats(dve, xin[0][:, :], B["st1"], B["mv1"], 1)
                dve_norm(dve, xin[0][:, :], B["mv1"], B["rs1"], B["nm1"], 1)
                dve_xn(dve, 1)
                dve_silu(dve, 1, 0)
                dve_silu(dve, 1, 1)

            @block.tensor
            def _(pe):
                pe_norm_t(pe, B["nm1"], B["tp1"], 1)
                pe_gate_bias(pe, G[0])
                for conv in (False, True):
                    for l in range(L):
                        pe_gates(pe, G[0], 1, l, conv)

        nums = sorted(s.num for s in sems)
        assert nums == list(range(nums[0], nums[0] + len(nums)))
        nc.gpsimd.sem_clear(range(nums[0], nums[0] + len(nums)))
        nc.all_engine_barrier()

        with nc.Fori(0, ITERS // 2) as it:
            with nc.Block() as block:
                @block.sync
                def _(sp):
                    for p in range(2):
                        new = xin[(p + 1) % 2]
                        sp.wait_ge(B["x2r"], p + 1)
                        sp.dma_start(new[Q:P, :], x2[0:P - Q, :]).then_inc(d_xin, 16)
                        sp.dma_start(scratch_out[bass.ds(it * (2 * CH) + p * CH, CH), :], x2[P - Q:P, :]).then_inc(d_out, 16)
                        sp.dma_start(new[0:Q, :], scratch_in[bass.ds(it * (2 * CH) + (p + 1) * CH, CH), :]).then_inc(d_xin, 16)
                    sp.wait_ge(d_xin, 64)
                    sp.wait_ge(d_out, 32)

                @block.gpsimd
                def _(pool):
                    for p in range(2):
                        k = p + 1
                        pool_heads(pool, xin[(p + 1) % 2][:, :], k)
                        pool_history(pool, it * 2 + (p + 1))
                        pool_conv(pool, k)
                        pool_silu(pool, k)

                @block.scalar
                def _(a):
                    s = nc.scalar

                    def beside(t, k):
                        if t == 3:
                            norm_scale(a, yvar[:, :], H, 1.0 / DH, eps_gn, B["yvar"], B["gln"], B["grs"], k)
                        if t == 6:
                            norm_scale(a, mv[:, 1:2], 1, 1.0, eps_ln, B["mv2"], B["ln2"], B["rs2"], k)
                        if t == 10:
                            act_gelu(a, k)
                        if t == 16:
                            norm_scale(a, mv[:, 1:2], 1, 1.0, eps_ln, B["mv1"], B["ln1"], B["rs1"], k)
                        if t == 21:
                            act_silu(a, k)

                    for p in range(2):
                        g = G[p]
                        for t in range(CH):
                            n = p * CH + t + 1
                            a.wait_ge(pre_ready, n)
                            s.activation(eb[:, :], g[Q:2 * Q, t, :], ACT.Exp, scale=1.0 / G_SCALE).then_inc(b_ready, 1)
                            s.activation(ex[:, 0:C], g[0:Q, t, :], ACT.Exp, scale=1.0 / G_SCALE)
                            s.activation(ex[:, C:2 * C], g[2 * Q:3 * Q, t, :], ACT.Exp, scale=1.0 / G_SCALE)
                            s.activation(ex[:, 2 * C:3 * C], g[3 * Q:P, t, :], ACT.Exp,
                                         scale=1.0 / G_SCALE).then_inc(gates_ready, 1)
                            a.wait_ge(t_ready, n)
                            s.activation(ll[:, 0:C], tt[:, 0:C], ACT.Ln)
                            s.activation(ll[:, C:2 * C], tt[:, 0:C], ACT.Ln, bias=1.0).then_inc(ln_ready, 1)
                            beside(t, p + 1)

                @block.tensor
                def _(pe):
                    def beside(t, p, k):
                        if t == 7:
                            pe_norm_t(pe, B["nm2"], B["tp2"], k)
                        if t in (8, 9):
                            mm = pe_up(pe, k, range((t - 8) * 2, (t - 8) * 2 + 2))
                            if t == 9:
                                mm.then_inc(B["upr"], 1)
                        if t == 11:
                            pe_gated_t(pe, k)
                        if t in (12, 13):
                            mm = pe_down(pe, k, range((t - 12) * 2, (t - 12) * 2 + 2))
                            if t == 13:
                                mm.then_inc(B["dnr"], 1)
                        if t == 14:
                            pe_gate_bias(pe, G[(p + 1) % 2])
                        if t == 17:
                            pe_norm_t(pe, B["nm1"], B["tp1"], k)
                        if 19 <= t < 19 + L:
                            pe_gates(pe, G[(p + 1) % 2], k, t - 19, False)
                        if 26 <= t < 26 + L:
                            pe_gates(pe, G[(p + 1) % 2], k, t - 26, True)

                    for p in range(2):
                        g = G[p]
                        for t in range(CH):
                            n = p * CH + t
                            if t == 0:
                                pe.wait_ge(B["ini"], p + 1)
                            else:
                                pe.wait_ge(h_split, n)
                            for c in range(C):
                                pe.matmul(g[:, t, c:c + 1], rec_w[:, c, :], st[:, c:c + 1],
                                          start=False, stop=False, skip_group_check=True)
                            if t:
                                pe.wait_ge(m_split, n)
                            pe.matmul(g[:, t, :], m_eye[:, :], ms[:, :],
                                      start=False, stop=True, skip_group_check=True).then_inc(pre_ready, 1)
                            beside(t, p, p + 1)

                @block.vector
                def _(dve):
                    v = nc.vector

                    def beside(t, p, k):
                        old = hb[(p + 1) % 2]
                        if t == 0:
                            dve_heads(dve, old)
                        if t == 1:
                            dve_head_sum(dve, k)
                        if t == 2:
                            dve_head_var(dve, k)
                        if t == 5:
                            dve.wait_ge(B["x1r"], k)
                            dve_stats(dve, x1[:, :], B["st2"], B["mv2"], k)
                        if t == 6:
                            dve_norm(dve, x1[:, :], B["mv2"], B["rs2"], B["nm2"], k)
                        if t == 7:
                            dve_n2(dve, k)
                        if t == 10:
                            dve_gated(dve, k)
                        if t == 11:
                            dve_gated_t(dve, k)
                        if t == 13:
                            dve_out(dve, k)
                        new = xin[(p + 1) % 2]
                        if t == 15:
                            dve.wait_ge(d_xin, 32 * k)
                            dve_stats(dve, new[:, :], B["st1"], B["mv1"], k)
                        if t == 16:
                            dve_norm(dve, new[:, :], B["mv1"], B["rs1"], B["nm1"], k)
                        if t == 17:
                            dve_xn(dve, k)
                        if t in (22, 23):
                            dve_silu(dve, k, t - 22)

                    for p in range(2):
                        c = it * 2 + p
                        m0 = 5 * p
                        if p:
                            dve.wait_ge(m_ready, CH)
                            dve.wait_ge(y_ready, CH)
                        v.tensor_tensor(m64[:, :], m64[:, :], keep_at(slice(0, Q), c), ALU.mult).then_inc(B["mks"], 1)
                        v.tensor_scalar(kb[:, :], keep_at(slice(0, Q), c), 1.0, -M_START * M_SCALE,
                                        ALU.subtract, ALU.mult).then_inc(B["mks"], 1)
                        v.tensor_tensor(hb[p][:, 0, C:2 * C], hb[1 - p][:, CH, C:2 * C], keep_at(slice(0, Q), c),
                                        ALU.mult)
                        if p:
                            dve.wait_ge(h_split, CH)
                        v.tensor_tensor(st[0:3 * Q, :], st[0:3 * Q, :], keep_at(slice(0, 3 * Q), c),
                                        ALU.mult).then_inc(B["mks"], 1)
                        dve.wait_ge(B["mks"], m0 + 3)
                        v.tensor_tensor(m64[:, :], m64[:, :], kb[:, :], ALU.add).then_inc(B["mks"], 1)
                        dve.wait_ge(B["mks"], m0 + 4)
                        v.tensor_copy(ms[0:Q, :], m64[:, :]).then_inc(B["mks"], 1)
                        dve.wait_ge(B["mks"], m0 + 5)
                        v.tensor_tensor(ms[Q:2 * Q, :], m64[:, :], ms[0:Q, :], ALU.subtract).then_inc(B["ini"], 1)

                        g, now = G[p], hb[p]
                        for t in range(CH):
                            n = p * CH + t + 1
                            dve.wait_ge(b_ready, n)
                            v.tensor_scalar(ad[:, 0:C], eb[:, :], E_TOP, LN_LOW, ALU.min, ALU.max).then_inc(bc_ready, 1)
                            dve.wait_ge(gates_ready, n)
                            dve.wait_ge(bc_ready, n)
                            v.scalar_tensor_tensor(out=tt[:, :], in0=ex[:, :], scalar=E_TOP, in1=ad[:, :],
                                                   op0=ALU.min, op1=ALU.add).then_inc(t_ready, 1)
                            s_, z1, o1 = tt[:, 0:C], tt[:, C:2 * C], tt[:, 2 * C:3 * C]
                            v.scalar_tensor_tensor(out=i64[:, :], in0=g[0:Q, t, :], scalar=M_SCALE / G_SCALE,
                                                   in1=m64[:, :], op0=ALU.mult, op1=ALU.add)
                            dve.wait_ge(t_ready, n)
                            v.scalar_tensor_tensor(out=p1[:, :], in0=s_, scalar=1.0, in1=z1,
                                                   op0=ALU.add, op1=ALU.mult).then_inc(p1_ready, 1)
                            v.tensor_tensor(a1[:, :], now[:, t, C:2 * C], z1, ALU.mult)
                            v.scalar_tensor_tensor(out=a2[:, :], in0=z1, scalar=-2.0, in1=s_,
                                                   op0=ALU.add, op1=ALU.mult).then_inc(a_ready, 1)
                            dve.wait_ge(p1_ready, n)
                            v.tensor_tensor(p2[:, :], p1[:, :], o1, ALU.mult).then_inc(p2_ready, 1)
                            dve.wait_ge(a_ready, n)
                            v.tensor_tensor(nn[:, :], a1[:, :], a2[:, :], ALU.add)
                            dve.wait_ge(p2_ready, n)
                            v.reciprocal(rp[:, :], p2[:, :]).then_inc(r_ready, 1)
                            dve.wait_ge(ln_ready, n)
                            v.tensor_tensor(vv[:, :], ll[:, C:2 * C], ll[:, 0:C], ALU.subtract)
                            dve.wait_ge(r_ready, n)
                            v.scalar_tensor_tensor(out=st[0:Q, :], in0=nn[:, :], scalar=H_SCALE, in1=rp[:, :],
                                                   op0=ALU.mult, op1=ALU.mult)
                            v.scalar_tensor_tensor(out=now[:, t + 1, 0:C], in0=nn[:, :], scalar=H_SCALE, in1=rp[:, :],
                                                   op0=ALU.mult, op1=ALU.mult).then_inc(h_ready, 1)
                            v.scalar_tensor_tensor(out=st[2 * Q:3 * Q, :], in0=nn[:, :], scalar=H_SCALE, in1=rp[:, :],
                                                   op0=ALU.mult, op1=ALU.mult)
                            dve.wait_ge(h_ready, n)
                            v.tensor_tensor(st[Q:2 * Q, :], now[:, t + 1, 0:C], st[0:Q, :],
                                            ALU.subtract).then_inc(h_split, 1)
                            v.scalar_tensor_tensor(out=ms[0:Q, :], in0=vv[:, :], scalar=M_SCALE, in1=i64[:, :],
                                                   op0=ALU.mult, op1=ALU.add)
                            v.scalar_tensor_tensor(out=m64[:, :], in0=vv[:, :], scalar=M_SCALE, in1=i64[:, :],
                                                   op0=ALU.mult, op1=ALU.add).then_inc(m_ready, 1)
                            v.scalar_tensor_tensor(out=now[:, t + 1, C:2 * C], in0=now[:, t + 1, 0:C],
                                                   scalar=1.0 / H_SCALE, in1=o1, op0=ALU.mult,
                                                   op1=ALU.mult).then_inc(y_ready, 1)
                            dve.wait_ge(m_ready, n)
                            v.tensor_tensor(ms[Q:2 * Q, :], m64[:, :], ms[0:Q, :], ALU.subtract).then_inc(m_split, 1)
                            beside(t, p, p + 1)

            nc.gpsimd.sem_clear(range(nums[0], nums[0] + len(nums)))
            nc.all_engine_barrier()

        with nc.Block() as block:
            @block.sync
            def _(sp):
                sp.wait_ge(B["x2r"], 1)
                sp.dma_start(scratch_out[ITERS * CH:(ITERS + 1) * CH, :], x2[P - Q:P, :]).then_inc(d_out, 16)
                sp.wait_ge(d_out, 16)

            @block.gpsimd
            def _(pool):
                pool_heads(pool, xin[(ITERS - 1) % 2][:, :], 1)

            @block.scalar
            def _(a):
                norm_scale(a, yvar[:, :], H, 1.0 / DH, eps_gn, B["yvar"], B["gln"], B["grs"], 1)
                norm_scale(a, mv[:, 1:2], 1, 1.0, eps_ln, B["mv2"], B["ln2"], B["rs2"], 1)
                act_gelu(a, 1)

            @block.tensor
            def _(pe):
                pe_norm_t(pe, B["nm2"], B["tp2"], 1)
                pe_up(pe, 1, range(L)).then_inc(B["upr"], 1)
                pe_gated_t(pe, 1)
                pe_down(pe, 1, range(L)).then_inc(B["dnr"], 1)

            @block.vector
            def _(dve):
                dve_heads(dve, hb[(ITERS - 1) % 2])
                dve_head_sum(dve, 1)
                dve_head_var(dve, 1)
                dve.wait_ge(B["x1r"], 1)
                dve_stats(dve, x1[:, :], B["st2"], B["mv2"], 1)
                dve_norm(dve, x1[:, :], B["mv2"], B["rs2"], B["nm2"], 1)
                dve_n2(dve, 1)
                dve_gated(dve, 1)
                dve_gated_t(dve, 1)
                dve_out(dve, 1)

        nc.gpsimd.sem_clear(range(nums[0], nums[0] + len(nums)))
        nc.all_engine_barrier()


def attention_stage(nc, x, ctx_in, w, scratch_out, first_row, att_out, xa_out, dims):
    S, D, HEADS, DHEAD, NK, DC = dims
    N = 512
    HALVES = S // N
    TILES = S // P
    KT = (NK + P - 1) // P
    LAST = NK - (KT - 1) * P
    SUB = N // P
    KC = [(i, min(i + 512, NK)) for i in range(0, NK, 512)]
    MX = SUB * len(KC)
    HEADS_A_PASS = 4
    GROUPS = HEADS_A_PASS * HALVES
    C_SCALE = 2.0 ** 4
    QK_SCALE = 2.0 ** 8
    S_SCALE = C_SCALE * QK_SCALE
    M_ONE = 2.0 ** 10
    LN_PROB = 10 * float(np.log(2.0))
    VC = 2 * DC + 1
    NS, NP_ = 3, 4

    with ExitStack() as ctx:
        def sb(name, shape, dt=F32, stack=ctx):
            return stack.enter_context(nc.sbuf_tensor(name, shape, dt))

        sems = []

        def sem(name):
            s = ctx.enter_context(nc.semaphore(name))
            sems.append(s)
            return s

        def ps(name, shape, dt=F32):
            return ctx.enter_context(nc.psum_tensor(name, shape, dt))

        identa = sb("identa", [P, P])
        keys_h = sb("keys_h", [DC + 1, KT * P], F16)
        keys_l = sb("keys_l", [DC, KT * P], F16)
        vals = sb("vals", [P, KT, VC], F16)
        qh = sb("qh", [DC + 1, (HEADS * HALVES + 1) * N], F16)
        ql = sb("ql", [DC, HEADS * HALVES * N], F16)
        vo_w = sb("vo_w", [DC, HEADS, D])
        ln_prob = sb("ln_prob", [P, 1])
        y_all = sb("y_all", [P, TILES, D])
        mx = sb("mx", [P, SUB, len(KC)])
        mxn = sb("mxn", [P, SUB])

        SC = [ps(f"SC{i}", [P, 512]) for i in range(NS)]
        MB = [ps(f"MB{i}", [P, 512]) for i in range(2)]
        OA = [ps(f"OA{i}", [P, 512]) for i in range(2)]
        XP = ps("XP", [P, 512])

        d_ctx, d_wt, d_x, d_y = (sem(n) for n in ("d_ctx", "d_wt", "d_x", "d_y"))
        c_zero, c_ident, w_t, w_tc, w_p, w_pc, k_t, k_hi, k_tc, v_hi = (
            sem(n) for n in ("c_zero", "c_ident", "w_t", "w_tc", "w_p", "w_pc", "k_t", "k_hi", "k_tc", "v_hi"))
        n_stat, n_mv, n_ln, n_rs, n_x, n_w, n_r, n_t, n_tc = (
            sem(n) for n in ("n_stat", "n_mv", "n_ln", "n_rs", "n_x", "n_w", "n_r", "n_t", "n_tc"))
        q_done, q_hi, q_copied = (sem(n) for n in ("q_done", "q_hi", "q_copied"))
        m_done, m_max, m_col, m_row, m_set = (sem(n) for n in ("m_done", "m_max", "m_col", "m_row", "m_set"))
        s_done, p_done, l_dve, l_pool, pv_done, o_free, o_rden, o_norm, o_sum = (
            sem(n) for n in ("s_done", "p_done", "l_dve", "l_pool", "pv_done", "o_free", "o_rden", "o_norm", "o_sum"))
        t_done, t_copied, y_done, y_added = (sem(n) for n in ("t_done", "t_copied", "y_done", "y_added"))
        nums = sorted(s.num for s in sems)
        assert nums == list(range(nums[0], nums[0] + len(nums)))

        with ExitStack() as c2:
            ctx_f = sb("ctx_f", [P, KT, DC], F32, c2)
            qk_w = sb("qk_w", [P, HEADS, DC], F32, c2)
            xat = sb("xat", [P, S], F32, c2)
            wq_sb = sb("wq_sb", [P, HEADS * DHEAD], F32, c2)
            wk_sb = sb("wk_sb", [DC, HEADS * DHEAD], F32, c2)
            wv_sb = sb("wv_sb", [DC, HEADS * DHEAD], F32, c2)
            wo_sb = sb("wo_sb", [DHEAD, HEADS, D], F32, c2)
            wt = sb("wt", [DHEAD, 3, P], F32, c2)
            post_w = sb("post_w", [P, D], F32, c2)
            eps_a = sb("eps_a", [P, 1], F32, c2)
            xs = sb("xs", [P, TILES, D], F32, c2)
            xo = sb("xo", [P, TILES, D], F32, c2)
            sta = sb("sta", [P, TILES, 6], F32, c2)
            mva = sb("mva", [P, TILES, 2], F32, c2)
            rsa = sb("rsa", [P, TILES], F32, c2)
            with nc.Block() as block:
                @block.sync
                def _(sp):
                    full = (KT - 1) * P
                    sp.dma_start(xs[:, :, :], scratch_out[first_row:first_row + S, :].rearrange("(j p) d -> p j d", p=P)).then_inc(d_x, 16)
                    sp.dma_start(xo[:, :, :], x.rearrange("(j p) d -> p j d", p=P)).then_inc(d_x, 16)
                    for dst, src in ((wq_sb[:, :], w["Wq"]), (wk_sb[:, :], w["Wk"]), (wv_sb[:, :], w["Wv"]),
                                     (wo_sb[:, :, :], w["Wo"].rearrange("(h i) n -> i h n", i=DHEAD)),
                                     (post_w[:, :], w["post_w"].unsqueeze(0).broadcast_to([P, D]))):
                        sp.dma_start(dst, src).then_inc(d_wt, 16)
                    sp.wait_ge(c_zero, 2)
                    sp.dma_start(ctx_f[:, 0:KT - 1, :], ctx_in[0:full, :].rearrange("(j p) d -> p j d", p=P)).then_inc(d_ctx, 16)
                    sp.dma_start(ctx_f[0:LAST, KT - 1, :], ctx_in[full:NK, :]).then_inc(d_ctx, 16)
                    sp.wait_ge(n_r, 2 * TILES)
                    sp.dma_start(xa_out.rearrange("(j p) d -> p j d", p=P), xo[:, :, :]).then_inc(d_y, 16)
                    sp.wait_ge(d_y, 16)

                @block.gpsimd
                def _(pool):
                    pool.memset(identa[:, :], 0.0).then_inc(c_zero, 1)
                    pool.memset(ctx_f[:, KT - 1, :], 0.0).then_inc(c_zero, 1)
                    pool.wait_ge(c_zero, 1)
                    pool.affine_select(out=identa[:, :], in_=identa[:, :], compare_op=ALU.not_equal, fill=1.0,
                                       base=0, pattern=[[-1, P]], channel_multiplier=1).then_inc(c_ident, 1)
                    pool.memset(vals[:, :, DC:DC + 1], 1.0)
                    pool.memset(y_all[:, :, :], 0.0)
                    pool.memset(qh[:, HEADS * HALVES * N:], 0.0)

                @block.scalar
                def _(a):
                    s = nc.scalar
                    s.preload_act_table_set("natural_log_exp_and_others")
                    a.wait_ge(d_ctx, 32)
                    s.activation(vals[:, :, 0:DC], ctx_f[:, :, :], ACT.Copy, scale=C_SCALE).then_inc(v_hi, 1)
                    for j in range(0, KT, 4):
                        n = min(4, KT - j)
                        a.wait_ge(k_t, j // 4 + 1)
                        s.activation(keys_h[0:DC, j * P:(j + n) * P], SC[(j // 4) % 2][0:DC, 0:n * P], ACT.Copy,
                                     scale=C_SCALE).then_inc(k_hi, 1)
                    for r in range(2):
                        a.wait_ge(n_mv, (r + 1) * TILES)
                        s.activation(rsa[:, :], mva[:, :, 1], ACT.Ln, bias=eps_a[:, 0:1]).then_inc(n_ln, 1)
                        a.wait_ge(n_ln, r + 1)
                        s.activation(rsa[:, :], rsa[:, :], ACT.Exp, scale=-0.5).then_inc(n_rs, 1)
                    for i in range(HEADS * HALVES):
                        a.wait_ge(q_done, i + 1)
                        s.activation(qh[0:DC, i * N:(i + 1) * N], SC[i % NS][0:DC, :], ACT.Copy).then_inc(q_hi, 1)

                @block.tensor
                def _(pe):
                    pe.wait_ge(c_ident, 1)
                    pe.wait_ge(d_wt, 16 * 5)
                    for h in range(HEADS):
                        if h:
                            pe.wait_ge(w_tc, h)
                        cols = slice(h * DHEAD, (h + 1) * DHEAD)
                        pe.transpose(MB[0][0:DHEAD, 0:P], wq_sb[:, cols], identa[:, :])
                        pe.transpose(MB[0][0:DHEAD, P:P + DC], wk_sb[:, cols], identa[0:DC, 0:DC])
                        pe.transpose(MB[0][0:DHEAD, 2 * P:2 * P + DC], wv_sb[:, cols], identa[0:DC, 0:DC]).then_inc(w_t, 1)
                        pe.wait_ge(w_tc, h + 1)
                        if h:
                            pe.wait_ge(w_pc, h)
                        pe.matmul(MB[1][:, 0:DC], wt[:, 0, :], wt[:, 1, 0:DC], start=True, stop=True)
                        pe.matmul(MB[1][0:DC, P:2 * P], wt[:, 2, 0:DC], wo_sb[:, h, :], start=True, stop=True).then_inc(w_p, 1)
                    pe.wait_ge(d_ctx, 32)
                    for j in range(0, KT, 4):
                        b = SC[(j // 4) % 2]
                        if j >= 8:
                            pe.wait_ge(k_tc, j // 4 - 1)
                        for i in range(j, min(j + 4, KT)):
                            mm = pe.transpose(b[0:DC, (i - j) * P:(i - j + 1) * P], ctx_f[:, i, :], identa[:, :])
                        mm.then_inc(k_t, 1)
                    for j in range(TILES):
                        pe.wait_ge(n_r, TILES + j + 1)
                        if j >= 2:
                            pe.wait_ge(n_tc, j - 1)
                        pe.transpose(OA[j % 2][:, 0:P], xo[:, j, :], identa[:, :]).then_inc(n_t, 1)
                    pe.wait_ge(k_tc, (KT + 3) // 4)
                    pe.wait_ge(w_pc, HEADS)
                    pe.wait_ge(n_tc, TILES)
                    for i in range(HEADS * HALVES):
                        if i >= NS:
                            pe.wait_ge(q_copied, i - NS + 1)
                        pe.matmul(SC[i % NS][0:DC, :], qk_w[:, i // HALVES, :], xat[:, (i % HALVES) * N:(i % HALVES + 1) * N],
                                  start=True, stop=True).then_inc(q_done, 1)

                @block.vector
                def _(dve):
                    v = nc.vector
                    v.memset(eps_a[:, :], EPS)
                    v.memset(keys_h[DC:DC + 1, :], M_ONE)
                    v.memset(ln_prob[:, :], LN_PROB).then_inc(n_w, 1)
                    for h in range(HEADS):
                        dve.wait_ge(w_t, h + 1)
                        v.tensor_copy(wt[:, 0, :], MB[0][0:DHEAD, 0:P])
                        v.tensor_copy(wt[:, 1:3, 0:DC], MB[0][0:DHEAD, P:3 * P].rearrange("p (a c) -> p a c", a=2)[:, :, 0:DC]).then_inc(w_tc, 1)
                        dve.wait_ge(w_p, h + 1)
                        v.tensor_scalar(qk_w[:, h, :], MB[1][:, 0:DC], QK_SCALE * float(DHEAD) ** -0.5, None, ALU.mult)
                        v.tensor_scalar(vo_w[:, h, :], MB[1][0:DC, P:2 * P], 1.0 / C_SCALE, None, ALU.mult).then_inc(w_pc, 1)
                    dve.wait_ge(v_hi, 1)
                    dve.wait_ge(d_ctx, 32)
                    v.scalar_tensor_tensor(out=vals[:, :, DC + 1:VC], in0=ctx_f[:, :, :], scalar=C_SCALE,
                                           in1=vals[:, :, 0:DC], op0=ALU.mult, op1=ALU.subtract)
                    for j in range(0, KT, 4):
                        n = min(4, KT - j)
                        dve.wait_ge(k_hi, j // 4 + 1)
                        v.scalar_tensor_tensor(out=keys_l[:, j * P:(j + n) * P], in0=SC[(j // 4) % 2][0:DC, 0:n * P],
                                               scalar=C_SCALE, in1=keys_h[0:DC, j * P:(j + n) * P],
                                               op0=ALU.mult, op1=ALU.subtract).then_inc(k_tc, 1)
                    dve.wait_ge(d_x, 32)
                    dve.wait_ge(d_wt, 16 * 5)
                    for r, buf in ((0, xs), (1, xo)):
                        if r:
                            dve.wait_ge(n_r, TILES)
                        for j in range(TILES):
                            v.bn_stats(sta[:, j, :], buf[:, j, :]).then_inc(n_stat, 1)
                        for j in range(TILES):
                            dve.wait_ge(n_stat, r * TILES + j + 1)
                            v.bn_aggr(mva[:, j, :], sta[:, j, :]).then_inc(n_mv, 1)
                        dve.wait_ge(n_mv, (r + 1) * TILES)
                        dve.wait_ge(n_rs, r + 1)
                        for j in range(TILES):
                            v.tensor_scalar(buf[:, j, :], buf[:, j, :], mva[:, j, 0:1], rsa[:, j:j + 1],
                                            ALU.subtract, ALU.mult).then_inc(n_r if r else n_x, 1)
                        if r == 0:
                            for j in range(TILES):
                                dve.wait_ge(n_x, j + 1)
                                v.tensor_tensor(xs[:, j, :], xs[:, j, :], post_w[:, :], ALU.mult).then_inc(n_w, 1)
                            for j in range(TILES):
                                dve.wait_ge(n_w, j + 2)
                                v.tensor_tensor(xo[:, j, :], xo[:, j, :], xs[:, j, :], ALU.add).then_inc(n_r, 1)
                    for j in range(TILES):
                        dve.wait_ge(n_t, j + 1)
                        v.tensor_copy(xat[:, j * P:(j + 1) * P], OA[j % 2][:, 0:P]).then_inc(n_tc, 1)
                    for i in range(HEADS * HALVES):
                        dve.wait_ge(q_hi, i + 1)
                        v.tensor_tensor(ql[:, i * N:(i + 1) * N], SC[i % NS][0:DC, :], qh[0:DC, i * N:(i + 1) * N],
                                        ALU.subtract).then_inc(q_copied, 1)

        def max_score(pe, first, n, done):
            a0, a1 = KC[n % len(KC)]
            if done + n >= 2:
                pe.wait_ge(m_max, done + n - 1)
            pe.matmul(MB[(done + n) % 2][:, 0:a1 - a0], qh[0:DC, bass.ds(first + (n // len(KC)) * P, P)],
                      keys_h[0:DC, a0:a1], start=True, stop=True).then_inc(m_done, 1)

        def max_reduce(dve, n, done):
            a0, a1 = KC[n % len(KC)]
            i = n // len(KC)
            dve.wait_ge(m_done, done + n + 1)
            nc.vector.tensor_reduce(mx[:, i, n % len(KC):n % len(KC) + 1], MB[(done + n) % 2][:, 0:a1 - a0],
                                    AX_X, ALU.max).then_inc(m_max, 1)

        def max_column(dve, k):
            dve.wait_ge(m_max, k * MX)
            nc.vector.tensor_reduce(mxn[:, :], mx[:, :, :], AX_X, ALU.max).then_inc(m_col, 1)

        def max_row(pe, k):
            pe.wait_ge(m_col, k)
            for i in range(SUB):
                mm = pe.matmul(XP[DC:DC + 1, i * P:(i + 1) * P], mxn[:, i:i + 1], identa[:, :], start=True, stop=True)
            mm.then_inc(m_row, 1)

        def max_set(dve, first, k):
            dve.wait_ge(m_row, k)
            nc.vector.tensor_scalar(qh[DC:DC + 1, bass.ds(first, N)], XP[DC:DC + 1, :], -1.0 / M_ONE, None,
                                    ALU.mult).then_inc(m_set, 1)

        nc.gpsimd.sem_clear(range(nums[0], nums[0] + len(nums)))
        nc.all_engine_barrier()
        with nc.Block() as block:
            @block.tensor
            def _(pe):
                for n in range(MX):
                    max_score(pe, 0, n, 0)
                max_row(pe, 1)

            @block.vector
            def _(dve):
                for n in range(MX):
                    max_reduce(dve, n, 0)
                max_column(dve, 1)
                max_set(dve, 0, 1)
        nc.gpsimd.sem_clear(range(nums[0], nums[0] + len(nums)))
        nc.all_engine_barrier()

        pf = sb("pf", [P, NP_, N])
        ph = sb("ph", [P, NP_, N], F16)
        pl = sb("pl", [P, NP_, N], F16)
        o_sb = sb("o_sb", [P, SUB, VC])
        o_n = sb("o_n", [P, SUB, DC])
        o_n2 = sb("o_n2", [P, SUB, DC])
        o_t = sb("o_t", [DC, N])
        rden = sb("rden", [P, SUB])
        TOTAL = GROUPS * KT
        EARLY = KT - 6
        T_NORM, T_TURN, T_TURNED, T_OUT, T_OUTED = 1, 4, 5, 7, 8
        T_ROW, T_SET = EARLY + 1, EARLY + 1

        def blocks(j):
            def upto(i):
                return min(MX, -(-i * MX // EARLY))
            return range(upto(j), upto(j + 1))

        def rows_of(j):
            return LAST if j == KT - 1 else P

        def by_vector(t):
            return t % 3 == 2

        with nc.Fori(0, HEADS // HEADS_A_PASS) as it:
            first = it * (GROUPS * N)
            with nc.Block() as block:
                @block.scalar
                def _(a):
                    s = nc.scalar
                    for t in range(TOTAL):
                        k = rows_of(t % KT)
                        if t >= NP_:
                            a.wait_ge(pv_done, t - NP_ + 1)
                        a.wait_ge(s_done, t + 1)
                        s.activation(ph[0:k, t % NP_, :], SC[t % NS][0:k, :], ACT.Exp, scale=1.0 / S_SCALE,
                                     bias=ln_prob[0:k, 0:1])
                        s.activation(pf[0:k, t % NP_, :], SC[t % NS][0:k, :], ACT.Exp, scale=1.0 / S_SCALE,
                                     bias=ln_prob[0:k, 0:1]).then_inc(p_done, 1)

                def low_part(eng, t):
                    k = rows_of(t % KT)
                    return eng.tensor_tensor(pl[0:k, t % NP_, :], pf[0:k, t % NP_, :], ph[0:k, t % NP_, :], ALU.subtract)

                @block.gpsimd
                def _(pool):
                    for t in range(TOTAL):
                        if not by_vector(t):
                            pool.wait_ge(p_done, t + 1)
                            low_part(nc.gpsimd, t).then_inc(l_pool, 1)

                @block.tensor
                def _(pe):
                    def scores(t):
                        g, j = divmod(t, KT)
                        k = rows_of(j)
                        if t >= NS:
                            pe.wait_ge(p_done, t - NS + 1)
                        if j == 0 and g:
                            pe.wait_ge(m_set, g)
                        out = SC[t % NS][0:k, :]
                        keys = slice(j * P, j * P + k)
                        at = bass.ds(first + g * N, N)
                        pe.matmul(out, keys_l[:, keys], qh[0:DC, at], start=True, stop=False)
                        pe.matmul(out, keys_h[0:DC, keys], ql[:, at], start=False, stop=False)
                        pe.matmul(out, keys_h[:, keys], qh[:, at], start=False, stop=True).then_inc(s_done, 1)

                    def turn(g):
                        pe.wait_ge(o_sum, SUB * (g + 1))
                        for i in range(SUB):
                            mm = pe.transpose(XP[0:DC, i * P:(i + 1) * P], o_n2[:, i, :], identa[:, :])
                        mm.then_inc(t_done, 1)

                    def project(g):
                        pe.wait_ge(t_copied, g + 1)
                        for i in range(SUB):
                            mm = pe.matmul(XP[:, i * P:(i + 1) * P], o_t[:, i * P:(i + 1) * P],
                                           vo_w[:, bass.ds(it * HEADS_A_PASS + g // HALVES, 1), :].rearrange("p a d -> p (a d)"),
                                           start=True, stop=True)
                        mm.then_inc(y_done, 1)

                    for t in range(NS):
                        scores(t)
                    for t in range(TOTAL):
                        g, j = divmod(t, KT)
                        k = rows_of(j)
                        for n in blocks(j):
                            max_score(pe, first + (g + 1) * N, n, g * MX)
                        if j == T_ROW:
                            if g:
                                pe.wait_ge(y_added, g)
                            max_row(pe, g + 1)
                        if g and j == T_TURN:
                            pe.wait_ge(m_set, g)
                            turn(g - 1)
                        if g and j == T_OUT:
                            project(g - 1)
                        pe.wait_ge(p_done, t + 1)
                        for i in range(SUB):
                            if j == 0 and g and i % 2 == 0:
                                pe.wait_ge(o_free, 2 * g - 1 + i // 2)
                            pe.matmul(OA[i // 2][:, (i % 2) * 256:(i % 2) * 256 + VC], ph[0:k, t % NP_, i * P:(i + 1) * P],
                                      vals[0:k, j, :], start=(j == 0 and i % 2 == 0), stop=False, skip_group_check=True)
                        if t + NS < TOTAL:
                            scores(t + NS)
                        if by_vector(t):
                            pe.wait_ge(l_dve, (t + 1) // 3)
                        else:
                            pe.wait_ge(l_pool, t + 1 - (t + 1) // 3)
                        for i in range(SUB):
                            mm = pe.matmul(OA[i // 2][:, (i % 2) * 256:(i % 2) * 256 + DC + 1], pl[0:k, t % NP_, i * P:(i + 1) * P],
                                           vals[0:k, j, 0:DC + 1], start=False, stop=(j == KT - 1), skip_group_check=True)
                        mm.then_inc(pv_done, 1)
                    pe.wait_ge(m_set, GROUPS)
                    turn(GROUPS - 1)
                    project(GROUPS - 1)

                @block.vector
                def _(dve):
                    v = nc.vector

                    def copy_sums(g):
                        dve.wait_ge(pv_done, KT * (g + 1))
                        for b in range(2):
                            v.tensor_copy(o_sb[:, 2 * b:2 * b + 2, :],
                                          OA[b][:, :].rearrange("p (a c) -> p a c", a=2)[:, :, 0:VC]).then_inc(o_free, 1)

                    def normalize(g):
                        dve.wait_ge(o_free, 2 * g + 2)
                        v.reciprocal(rden[:, :], o_sb[:, :, DC]).then_inc(o_rden, 1)
                        dve.wait_ge(o_rden, g + 1)
                        for i in range(SUB):
                            v.tensor_scalar(o_n[:, i, :], o_sb[:, i, 0:DC], rden[:, i:i + 1], None, ALU.mult).then_inc(o_norm, 1)
                        for i in range(SUB):
                            dve.wait_ge(o_norm, SUB * g + i + 1)
                            v.scalar_tensor_tensor(out=o_n2[:, i, :], in0=o_sb[:, i, DC + 1:VC], scalar=rden[:, i:i + 1],
                                                   in1=o_n[:, i, :], op0=ALU.mult, op1=ALU.add).then_inc(o_sum, 1)

                    def copy_turned(g):
                        dve.wait_ge(t_done, g + 1)
                        v.tensor_copy(o_t[:, :], XP[0:DC, :]).then_inc(t_copied, 1)

                    def add_out(g):
                        h0 = (g % HALVES) * SUB
                        dve.wait_ge(y_done, g + 1)
                        if g >= HALVES:
                            dve.wait_ge(y_added, g - HALVES + 1)
                        y = y_all[:, h0:h0 + SUB, :].rearrange("p a d -> p (a d)")
                        v.tensor_tensor(y, XP[:, :], y, ALU.add).then_inc(y_added, 1)

                    for t in range(TOTAL):
                        g, j = divmod(t, KT)
                        if by_vector(t + 1) and t + 1 < TOTAL:
                            dve.wait_ge(p_done, t + 2)
                            low_part(v, t + 1).then_inc(l_dve, 1)
                        if g and j == 0:
                            copy_sums(g - 1)
                        for n in blocks(j):
                            max_reduce(dve, n, g * MX)
                        if g and j == T_NORM:
                            normalize(g - 1)
                        if g and j == T_TURNED:
                            copy_turned(g - 1)
                        if g and j == T_OUTED:
                            add_out(g - 1)
                        if j == EARLY:
                            max_column(dve, g + 1)
                        if j == T_SET:
                            max_set(dve, first + (g + 1) * N, g + 1)
                    copy_sums(GROUPS - 1)
                    normalize(GROUPS - 1)
                    copy_turned(GROUPS - 1)
                    add_out(GROUPS - 1)

            nc.gpsimd.sem_clear(range(nums[0], nums[0] + len(nums)))
            nc.all_engine_barrier()

        with nc.Block() as block:
            @block.sync
            def _(sp):
                sp.dma_start(att_out.rearrange("(j p) d -> p j d", p=P), y_all[:, :, :]).then_inc(d_y, 16)
                sp.wait_ge(d_y, 16)
        nc.gpsimd.sem_clear(range(nums[0], nums[0] + len(nums)))
        nc.all_engine_barrier()


def experts_stage(nc, att, xa, w, bo, row_p, row_i, out, dims):
    S, D, E, FF, CAP = dims
    TILES = S // P
    FC = FF // P
    HALF = 512
    with ExitStack() as ctx:
        def sb(name, shape, dt=F32):
            return ctx.enter_context(nc.sbuf_tensor(name, shape, dt))

        def sem(name):
            return ctx.enter_context(nc.semaphore(name))

        def ps(name, shape, dt=F32):
            return ctx.enter_context(nc.psum_tensor(name, shape, dt))

        idente = sb("idente", [P, P])
        w1 = sb("w1", [P, E, FF])
        w2 = sb("w2", [P, E, FC, D])
        b1n = sb("b1n", [E * FC, P])
        b1t = sb("b1t", [P, E * FC])
        b2r = sb("b2r", [1, E, D])
        ones = sb("ones", [1, P])
        rwn = sb("rwn", [E, D])
        rwt = sb("rwt", [P, E])
        bo_r = sb("bo_r", [P, D])
        eps_e = sb("eps_e", [P, 1])
        xb = sb("xb", [P, TILES, D])
        ya = sb("ya", [P, TILES, D])
        xbt = sb("xbt", [P, S])
        lg = sb("lg", [P, TILES, E])
        le = sb("le", [P, TILES, E])
        lmax = sb("lmax", [P, TILES])
        lsum = sb("lsum", [P, TILES])
        prob = sb("prob", [P, TILES])
        cand = sb("cand", [P, TILES, E])
        weigh = sb("weigh", [P, E])
        idx = sb("idx", [P, TILES])
        prow = sb("prow", [P, S])
        irow = sb("irow", [P, S])
        before = sb("before", [P, 2 * S])
        beat = sb("beat", [P, S])
        tie = sb("tie", [P, S])
        rank = sb("rank", [P, TILES])
        kept = sb("kept", [P, TILES])
        fin_e = sb("fin_e", [P, TILES])
        mask = sb("mask", [P, TILES, E])
        hid = sb("hid", [P, 2, FC, S])
        acc = sb("acc", [P, TILES, D])
        st_e = sb("st_e", [P, TILES, 6])
        mv_e = sb("mv_e", [P, TILES, 2])
        rs_e = sb("rs_e", [P, TILES])
        HP = [ps(f"HP{i}", [P, 512]) for i in range(4)]
        YE = [ps(f"YE{i}", [P, 512]) for i in range(2)]
        TE = [ps(f"TE{i}", [P, 512]) for i in range(2)]

        e_w, e_w2, e_x, e_row, e_out, e_sc = (sem(n) for n in ("e_w", "e_w2", "e_x", "e_row", "e_out", "e_sc"))
        e_id, e_z, e_wg, e_bt, e_btc = (sem(n) for n in ("e_id", "e_z", "e_wg", "e_bt", "e_btc"))
        e_add, e_add2, e_st, e_mv, e_ln, e_rs, e_xb, e_t, e_tc, e_lg, e_lgc = (
            sem(n) for n in ("e_add", "e_add2", "e_st", "e_mv", "e_ln", "e_rs", "e_xb", "e_t", "e_tc", "e_lg", "e_lgc"))
        e_max, e_exp, e_sum, e_p, e_c, e_c2, e_i0, e_i, e_g, e_tie, e_b, e_rk, e_kp, e_fe, e_mk = (
            sem(n) for n in ("e_max", "e_exp", "e_sum", "e_p", "e_c", "e_c2", "e_i0", "e_i", "e_g", "e_tie", "e_b", "e_rk", "e_kp", "e_fe", "e_mk"))
        e_h, e_hr, e_y, e_ya, e_fin, e_st2, e_mv2, e_ln2, e_rs2 = (
            sem(n) for n in ("e_h", "e_hr", "e_y", "e_ya", "e_fin", "e_st2", "e_mv2", "e_ln2", "e_rs2"))
        NW = 4

        with nc.Block() as block:
            @block.sync
            def _(sp):
                sp.dma_start(xb[:, :, :], xa.rearrange("(j p) d -> p j d", p=P)).then_inc(e_x, 16)
                sp.dma_start(ya[:, :, :], att.rearrange("(j p) d -> p j d", p=P)).then_inc(e_x, 16)
                sp.dma_start(bo_r[:, :], bo.unsqueeze(0).broadcast_to([P, D])).then_inc(e_w, 16)
                sp.dma_start(rwn[:, :], w["router_w"]).then_inc(e_w, 16)
                sp.dma_start(b1n[:, :], w["b1"].rearrange("e (c p) -> (e c) p", p=P)).then_inc(e_w, 16)
                sp.dma_start(b2r[:, :, :], w["b2"].unsqueeze(0)).then_inc(e_w, 16)
                for e in range(E):
                    sp.dma_start(w1[:, e, :], w["W1"][e]).then_inc(e_w2, 16)
                    sp.dma_start(w2[:, e, :, :], w["W2"][e].rearrange("(c p) d -> p c d", p=P)).then_inc(e_w2, 16)
                sp.wait_ge(e_p, 1)
                sp.wait_ge(e_i, 1)
                sp.dma_start(row_p.rearrange("(j p) -> p j", p=P), prob[:, :], allow_slow_non_contiguous=True).then_inc(e_sc, 16)
                sp.dma_start(row_i.rearrange("(j p) -> p j", p=P), idx[:, :], allow_slow_non_contiguous=True).then_inc(e_sc, 16)
                sp.wait_ge(e_sc, 32)
                sp.dma_start(prow[:, :], row_p.unsqueeze(0).broadcast_to([P, S])).then_inc(e_row, 16)
                sp.dma_start(irow[:, :], row_i.unsqueeze(0).broadcast_to([P, S])).then_inc(e_row, 16)
                sp.wait_ge(e_fin, TILES)
                sp.dma_start(out.rearrange("(j p) d -> p j d", p=P), acc[:, :, :]).then_inc(e_out, 16)
                sp.wait_ge(e_out, 16)

            @block.gpsimd
            def _(pool):
                pool.memset(idente[:, :], 0.0).then_inc(e_z, 1)
                pool.memset(before[:, :], 1.0).then_inc(e_z, 1)
                pool.wait_ge(e_z, 2)
                pool.affine_select(out=idente[:, :], in_=idente[:, :], compare_op=ALU.not_equal, fill=1.0,
                                   base=0, pattern=[[-1, P]], channel_multiplier=1).then_inc(e_id, 1)
                pool.affine_select(out=before[:, :], in_=before[:, :], compare_op=ALU.is_gt, fill=0.0,
                                   base=S, pattern=[[-1, 2 * S]], channel_multiplier=1).then_inc(e_id, 1)

            @block.scalar
            def _(a):
                s = nc.scalar
                s.preload_act_table_set("natural_log_exp_and_others")
                for j in range(TILES):
                    a.wait_ge(e_mv, j + 1)
                    s.activation(rs_e[:, j:j + 1], mv_e[:, j, 1:2], ACT.Ln, bias=eps_e[:, 0:1]).then_inc(e_ln, 1)
                    a.wait_ge(e_ln, j + 1)
                    s.activation(rs_e[:, j:j + 1], rs_e[:, j:j + 1], ACT.Exp, scale=-0.5).then_inc(e_rs, 1)
                a.wait_ge(e_max, 2)
                s.activation(le[:, :, :], le[:, :, :], ACT.Exp).then_inc(e_exp, 1)
                a.wait_ge(e_btc, 1)
                for e in range(E):
                    if e >= 2:
                        a.wait_ge(e_y, (e - 1) * TILES)
                    for c in range(FC):
                        for h in range(S // HALF):
                            n = (e * FC + c) * 2 + h
                            a.wait_ge(e_h, n + 1)
                            s.activation(hid[:, e % 2, c, h * HALF:(h + 1) * HALF], HP[n % 4][:, :], ACT.Relu,
                                         bias=b1t[:, e * FC + c:e * FC + c + 1]).then_inc(e_hr, 1)
                for j in range(TILES):
                    a.wait_ge(e_mv2, j + 1)
                    s.activation(rs_e[:, j:j + 1], mv_e[:, j, 1:2], ACT.Ln, bias=eps_e[:, 0:1]).then_inc(e_ln2, 1)
                    a.wait_ge(e_ln2, j + 1)
                    s.activation(rs_e[:, j:j + 1], rs_e[:, j:j + 1], ACT.Exp, scale=-0.5).then_inc(e_rs2, 1)

            @block.tensor
            def _(pe):
                pe.wait_ge(e_id, 1)
                pe.wait_ge(e_w, 16 * NW)
                pe.transpose(TE[0][:, 0:E], rwn[:, :], idente[0:E, 0:E])
                pe.transpose(TE[0][:, E:E + E * FC], b1n[:, :], idente[0:E * FC, 0:E * FC]).then_inc(e_bt, 1)
                for j in range(TILES):
                    pe.wait_ge(e_xb, j + 1)
                    if j >= 2:
                        pe.wait_ge(e_tc, j - 1)
                    else:
                        pe.wait_ge(e_btc, 1)
                    pe.transpose(TE[j % 2][:, 0:P], xb[:, j, :], idente[:, :]).then_inc(e_t, 1)
                pe.wait_ge(e_tc, TILES)
                for j in range(TILES):
                    mm = pe.matmul(YE[0][:, j * E:(j + 1) * E], xbt[:, j * P:(j + 1) * P], rwt[:, :], start=True, stop=True)
                mm.then_inc(e_lg, 1)

                def hidden(e):
                    pe.wait_ge(e_w2, 32 * E)
                    for c in range(FC):
                        for h in range(S // HALF):
                            n = (e * FC + c) * 2 + h
                            if n >= 4:
                                pe.wait_ge(e_hr, n - 3)
                            pe.matmul(HP[n % 4][:, :], w1[:, e, c * P:(c + 1) * P], xbt[:, h * HALF:(h + 1) * HALF],
                                      start=True, stop=True).then_inc(e_h, 1)

                hidden(0)
                pe.wait_ge(e_lgc, 1)
                for e in range(E):
                    if e + 1 < E:
                        hidden(e + 1)
                    pe.wait_ge(e_hr, (e + 1) * FC * 2)
                    for j in range(TILES):
                        n = e * TILES + j
                        if n >= 2:
                            pe.wait_ge(e_ya, n - 1)
                        pe.matmul(YE[n % 2][:, 0:D], ones[:, :], b2r[:, e, :], start=True, stop=False)
                        for c in range(FC):
                            mm = pe.matmul(YE[n % 2][:, 0:D], hid[:, e % 2, c, j * P:(j + 1) * P], w2[:, e, c, :],
                                           start=False, stop=(c == FC - 1))
                        mm.then_inc(e_y, 1)

            @block.vector
            def _(dve):
                v = nc.vector
                v.memset(eps_e[:, :], EPS)
                v.memset(ones[:, :], 1.0).then_inc(e_wg, 1)
                for e in range(E):
                    v.memset(weigh[:, e:e + 1], float(E - e)).then_inc(e_wg, 1)
                dve.wait_ge(e_bt, 1)
                v.tensor_copy(rwt[:, :], TE[0][:, 0:E])
                v.tensor_copy(b1t[:, :], TE[0][:, E:E + E * FC]).then_inc(e_btc, 1)
                dve.wait_ge(e_x, 32)
                dve.wait_ge(e_w, 16 * NW)
                for j in range(TILES):
                    v.tensor_tensor(ya[:, j, :], ya[:, j, :], bo_r[:, :], ALU.add).then_inc(e_add, 1)
                    dve.wait_ge(e_add, j + 1)
                    v.tensor_tensor(xb[:, j, :], xb[:, j, :], ya[:, j, :], ALU.add).then_inc(e_add2, 1)
                    dve.wait_ge(e_add2, j + 1)
                    v.bn_stats(st_e[:, j, :], xb[:, j, :]).then_inc(e_st, 1)
                    dve.wait_ge(e_st, j + 1)
                    v.bn_aggr(mv_e[:, j, :], st_e[:, j, :]).then_inc(e_mv, 1)
                for j in range(TILES):
                    dve.wait_ge(e_mv, j + 1)
                    dve.wait_ge(e_rs, j + 1)
                    v.tensor_scalar(xb[:, j, :], xb[:, j, :], mv_e[:, j, 0:1], rs_e[:, j:j + 1],
                                    ALU.subtract, ALU.mult).then_inc(e_xb, 1)
                for j in range(TILES):
                    dve.wait_ge(e_t, j + 1)
                    v.tensor_copy(xbt[:, j * P:(j + 1) * P], TE[j % 2][:, 0:P]).then_inc(e_tc, 1)
                dve.wait_ge(e_lg, 1)
                v.tensor_copy(lg[:, :, :].rearrange("p j e -> p (j e)"), YE[0][:, 0:TILES * E]).then_inc(e_lgc, 1)
                dve.wait_ge(e_lgc, 1)
                v.tensor_reduce(lmax[:, :], lg[:, :, :], AX_X, ALU.max).then_inc(e_max, 1)
                dve.wait_ge(e_max, 1)
                mb = lmax[:, :].unsqueeze(2).broadcast_to([P, TILES, E])
                v.tensor_tensor(le[:, :, :], lg[:, :, :], mb, ALU.subtract).then_inc(e_max, 1)
                v.tensor_tensor(cand[:, :, :], lg[:, :, :], mb, ALU.is_ge).then_inc(e_c, 1)
                dve.wait_ge(e_c, 1)
                v.tensor_tensor(cand[:, :, :], cand[:, :, :], weigh[:, :].unsqueeze(1).broadcast_to([P, TILES, E]),
                                ALU.mult).then_inc(e_c2, 1)
                dve.wait_ge(e_c2, 1)
                v.tensor_reduce(idx[:, :], cand[:, :, :], AX_X, ALU.max).then_inc(e_i0, 1)
                dve.wait_ge(e_i0, 1)
                v.tensor_scalar(idx[:, :], idx[:, :], -1.0, float(E), ALU.mult, ALU.add).then_inc(e_i, 1)
                dve.wait_ge(e_exp, 1)
                v.tensor_reduce(lsum[:, :], le[:, :, :], AX_X, ALU.add).then_inc(e_sum, 1)
                dve.wait_ge(e_sum, 1)
                v.reciprocal(prob[:, :], lsum[:, :]).then_inc(e_p, 1)
                dve.wait_ge(e_row, 32)
                dve.wait_ge(e_p, 1)
                dve.wait_ge(e_id, 2)
                for j in range(TILES):
                    if j:
                        dve.wait_ge(e_rk, j)
                    v.tensor_scalar(beat[:, :], prow[:, :], prob[:, j:j + 1], None, ALU.is_gt).then_inc(e_g, 1)
                    v.scalar_tensor_tensor(out=tie[:, :], in0=prow[:, :], scalar=prob[:, j:j + 1],
                                           in1=before[:, S - j * P:2 * S - j * P], op0=ALU.is_equal,
                                           op1=ALU.mult).then_inc(e_tie, 1)
                    dve.wait_ge(e_tie, j + 1)
                    v.tensor_tensor(beat[:, :], beat[:, :], tie[:, :], ALU.add).then_inc(e_b, 1)
                    dve.wait_ge(e_b, j + 1)
                    v.scalar_tensor_tensor(out=tie[:, :], in0=irow[:, :], scalar=idx[:, j:j + 1], in1=beat[:, :],
                                           op0=ALU.is_equal, op1=ALU.mult, accum_out=rank[:, j:j + 1]).then_inc(e_rk, 1)
                dve.wait_ge(e_rk, TILES)
                v.tensor_scalar(kept[:, :], rank[:, :], float(CAP), None, ALU.is_lt).then_inc(e_kp, 1)
                dve.wait_ge(e_kp, 1)
                v.tensor_tensor(fin_e[:, :], idx[:, :], kept[:, :], ALU.mult).then_inc(e_fe, 1)
                dve.wait_ge(e_fe, 1)
                for e in range(E):
                    ins = v.tensor_scalar(mask[:, :, e], fin_e[:, :], float(e), None, ALU.is_equal)
                ins.then_inc(e_mk, 1)
                dve.wait_ge(e_mk, 1)
                for e in range(E):
                    for j in range(TILES):
                        n = e * TILES + j
                        dve.wait_ge(e_y, n + 1)
                        if e:
                            dve.wait_ge(e_ya, n - TILES + 1)
                        v.scalar_tensor_tensor(out=acc[:, j, :], in0=YE[n % 2][:, 0:D], scalar=mask[:, j, e:e + 1],
                                               in1=acc[:, j, :] if e else xb[:, j, :],
                                               op0=ALU.mult, op1=ALU.add).then_inc(e_ya, 1)
                for j in range(TILES):
                    dve.wait_ge(e_ya, (E - 1) * TILES + j + 1)
                    v.bn_stats(st_e[:, j, :], acc[:, j, :]).then_inc(e_st2, 1)
                    dve.wait_ge(e_st2, j + 1)
                    v.bn_aggr(mv_e[:, j, :], st_e[:, j, :]).then_inc(e_mv2, 1)
                for j in range(TILES):
                    dve.wait_ge(e_mv2, j + 1)
                    dve.wait_ge(e_rs2, j + 1)
                    v.tensor_scalar(acc[:, j, :], acc[:, j, :], mv_e[:, j, 0:1], rs_e[:, j:j + 1],
                                    ALU.subtract, ALU.mult).then_inc(e_fin, 1)


_INS = ["x", "ctx_768", "L0_attn_ln1_w", "L0_attn_conv_w", "L0_attn_conv_b", "L0_attn_wi", "L0_attn_wf", "L0_attn_wz",
        "L0_attn_wo", "L0_attn_rker", "L0_attn_cell_b", "L0_attn_gn_w", "L0_attn_ln2_w", "L0_attn_ff_up",
        "L0_attn_ff_down", "L0_attn_post_w", "L0_xattn_Wq", "L0_xattn_Wk", "L0_xattn_Wv", "L0_xattn_Wo",
        "L0_xattn_bo", "L0_ffn_router_w", "L0_ffn_W1", "L0_ffn_b1", "L0_ffn_W2", "L0_ffn_b2"]


def decoder_kernel(nc, t, out):
    _, S, D = t["x"].shape
    NK, DC = t["ctx_768"].shape[1:]
    L, H, DH, _ = t["L0_attn_wi"].shape
    K = t["L0_attn_conv_w"].shape[2]
    UP = t["L0_attn_ff_down"].shape[1]
    E, _, FF = t["L0_ffn_W1"].shape
    DHEAD = 64
    HEADS = t["L0_xattn_Wq"].shape[1] // DHEAD
    rows = S + (2 * (L - 1) + 1) * Q
    x = t["x"].rearrange("b s d -> (b s) d")
    scr_in = nc.dram_tensor("scr_in", [rows + Q, D], F32).ap()
    scr_out = nc.dram_tensor("scr_out", [rows, D], F32).ap()
    xa = nc.dram_tensor("scr_xa", [S, D], F32).ap()
    att = nc.dram_tensor("scr_att", [S, D], F32).ap()
    row_p = nc.dram_tensor("scr_p", [S], F32).ap()
    row_i = nc.dram_tensor("scr_i", [S], F32).ap()
    slstm_stage(nc, x, {n[8:]: t[n] for n in _INS if n.startswith("L0_attn_")}, scr_in, scr_out,
                (S, D, L, H, K, UP))
    xw = {n[9:]: t[n] for n in _INS if n.startswith("L0_xattn_")}
    xw["post_w"] = t["L0_attn_post_w"]
    attention_stage(nc, x, t["ctx_768"].rearrange("b s d -> (b s) d"), xw, scr_out, rows - S, att, xa,
                    (S, D, HEADS, DHEAD, NK, DC))
    capacity = -(-S * 5 // (4 * E))
    experts_stage(nc, att, xa, {n[7:]: t[n] for n in _INS if n.startswith("L0_ffn_")}, t["L0_xattn_bo"],
                  row_p, row_i, out.rearrange("b s d -> (b s) d"), (S, D, E, FF, capacity))


def kernel(**inputs):
    from concourse import bacc
    from concourse.bass_utils import run_bass_kernel_spmd

    nc = bacc.Bacc("TRN2", target_bir_lowering=False, num_devices=1)
    arrays, t = {}, {}
    for name in _INS:
        a = np.ascontiguousarray(inputs[name])
        arrays["in_" + name] = a
        t[name] = nc.dram_tensor("in_" + name, a.shape, mybir.dt.from_np(a.dtype), kind="ExternalInput").ap()
    out = nc.dram_tensor("out_dram", t["x"].shape, F32, kind="ExternalOutput").ap()
    decoder_kernel(nc, t, out)
    r = run_bass_kernel_spmd(nc, [arrays], core_ids=[0])
    return r.results[0]["out_dram"]
```
